# Optimizing a Trainium2 kernel written in Bass

```python
import numpy as np
import jax
import jax.numpy as jnp

def _softmax(x, axis=-1):
    return jax.nn.softmax(x, axis=axis)

def _gelu(x):
    return jax.nn.gelu(x, approximate=True)

def _silu(x):
    return jax.nn.silu(x)

def _sigmoid(x):
    return jax.nn.sigmoid(x)

def _layernorm(x, axis=-1, eps=1e-05):
    m = jnp.mean(x, axis=axis, keepdims=True)
    v = jnp.var(x, axis=axis, keepdims=True)
    return (x - m) / jnp.sqrt(v + eps)

def _scatter_add(tgt, idx, src, axis=0):
    return tgt.at[idx].add(src)

def _segment_sum(src, seg, n):
    return jax.ops.segment_sum(src, seg, n)
kernel_name = 'mk_adj_resnorm_d2_adj_r2_db59bc'

def setup_inputs(seed: int=0):
    np.random.seed(seed)
    _w = jnp.asarray

    def _rec_inputs():
        import jax
        import jax.numpy as jnp
        _gk = jax.random.key(seed)
        x = -0.000929 + 1 * jax.random.normal(jax.random.fold_in(_gk, 1), (16, 512, 128), jnp.float32)
        _w = (1.0 + jnp.arange(512, dtype=jnp.float32)) ** (-0.5)
        _w = _w / _w.mean()
        _pij = jnp.clip(0.03125 * _w[:, None] * _w[None, :], 0.0, 1.0)
        _a = jax.random.uniform(jax.random.fold_in(_gk, 2), (16, 512, 512)) < _pij
        _af = _a.astype(jnp.float32)
        adj = _af
        return (x, adj)
    x, adj = _rec_inputs()

    def _L0_gnn_setup():
        import jax, jax.numpy as jnp
        import numpy as np
        B, N, F_IN, H, D = (8, 512, 128, 4, 32)
        NEG_SLOPE = 0.2
        EDGE_PROB = 0.03
        key = jax.random.key(seed)
        ks = jax.random.split(key, 8)
        inputs = jax.random.normal(ks[0], (B, N, F_IN), dtype=jnp.float32)
        adj_mat = (jax.random.uniform(ks[1], (B, N, N)) < EDGE_PROB).astype(jnp.float32)
        stdv = 1.0 / np.sqrt(H * D)
        weight = jax.random.uniform(ks[2], (F_IN, H * D), minval=-stdv, maxval=stdv, dtype=jnp.float32)
        bias = jax.random.uniform(ks[3], (1, H * D), minval=-stdv, maxval=stdv, dtype=jnp.float32)
        weight_u = jax.random.uniform(ks[4], (H, D, 1), minval=-1.0, maxval=1.0, dtype=jnp.float32)
        weight_v = jax.random.uniform(ks[5], (H, D, 1), minval=-1.0, maxval=1.0, dtype=jnp.float32)
        pstd = 1.0 / np.sqrt(F_IN)
        proj_w = jax.random.uniform(ks[6], (H * D, F_IN), minval=-pstd, maxval=pstd, dtype=jnp.float32)
        proj_b = jax.random.uniform(ks[7], (H * D,), minval=-pstd, maxval=pstd, dtype=jnp.float32)
        return {'inputs': inputs, 'adj_mat': adj_mat, 'weight': weight, 'weight_u': weight_u, 'weight_v': weight_v, 'bias': bias, 'proj_w': proj_w, 'proj_b': proj_b}
    _L0_gnn_all = _L0_gnn_setup()
    _L0_gnn_in = {k: v for k, v in _L0_gnn_all.items() if k in ('weight', 'weight_u', 'weight_v', 'bias', 'proj_w', 'proj_b')}
    del _L0_gnn_all

    def _L1_gnn_setup():
        import jax, jax.numpy as jnp
        import numpy as np
        B, N, DIN, HID = (8, 1024, 128, 128)
        CLAMP_HI = 90000000000000.0
        NEG_PENALTY = 9000000000000000.0
        key = jax.random.key(seed)
        ks = jax.random.split(key, 8)
        s = 1.0 / np.sqrt(DIN)
        x = jax.random.normal(ks[0], (B, N, DIN), dtype=jnp.float32)
        mask = jax.random.randint(ks[1], (B, N, N), 0, 2).astype(jnp.float32)
        Wv = jax.random.uniform(ks[2], (HID, DIN), jnp.float32, -s, s)
        bv = jax.random.uniform(ks[3], (HID,), jnp.float32, -s, s)
        Wk = jax.random.uniform(ks[4], (HID, DIN), jnp.float32, -s, s)
        bk = jax.random.uniform(ks[5], (HID,), jnp.float32, -s, s)
        Wq = jax.random.uniform(ks[6], (HID, DIN), jnp.float32, -s, s)
        bq = jax.random.uniform(ks[7], (HID,), jnp.float32, -s, s)
        return {'x': x, 'mask': mask, 'Wv': Wv, 'bv': bv, 'Wk': Wk, 'bk': bk, 'Wq': Wq, 'bq': bq}
    _L1_gnn_all = _L1_gnn_setup()
    _L1_gnn_in = {k: v for k, v in _L1_gnn_all.items() if k in ('Wv', 'bv', 'Wk', 'bk', 'Wq', 'bq')}
    del _L1_gnn_all
    return {'x': x, 'adj': adj, 'L0_gnn_weight': _L0_gnn_in['weight'], 'L0_gnn_weight_u': _L0_gnn_in['weight_u'], 'L0_gnn_weight_v': _L0_gnn_in['weight_v'], 'L0_gnn_bias': _L0_gnn_in['bias'], 'L0_gnn_proj_w': _L0_gnn_in['proj_w'], 'L0_gnn_proj_b': _L0_gnn_in['proj_b'], 'L1_gnn_Wv': _L1_gnn_in['Wv'], 'L1_gnn_bv': _L1_gnn_in['bv'], 'L1_gnn_Wk': _L1_gnn_in['Wk'], 'L1_gnn_bk': _L1_gnn_in['bk'], 'L1_gnn_Wq': _L1_gnn_in['Wq'], 'L1_gnn_bq': _L1_gnn_in['bq']}

def reference(x, adj, L0_gnn_weight, L0_gnn_weight_u, L0_gnn_weight_v, L0_gnn_bias, L0_gnn_proj_w, L0_gnn_proj_b, L1_gnn_Wv, L1_gnn_bv, L1_gnn_Wk, L1_gnn_bk, L1_gnn_Wq, L1_gnn_bq):
    import jax
    import jax.numpy as jnp

    def _L0_gnn_ref(inputs, adj_mat, weight, weight_u, weight_v, bias, proj_w, proj_b):
        import jax, jax.numpy as jnp
        import numpy as np
        B, N, F_IN, H, D = (8, 512, 128, 4, 32)
        NEG_SLOPE = 0.2
        EDGE_PROB = 0.03
        b, n, _ = inputs.shape
        row_zero = jnp.all(adj_mat == 0, axis=-1, keepdims=True)
        adj = jnp.where(row_zero, jnp.float32(1e-06), adj_mat)
        support = (inputs @ weight).reshape(b, n, H, D).transpose(0, 2, 1, 3)
        f1 = jnp.einsum('bhnd,hd->bhn', support, weight_u[..., 0])[:, :, None, :]
        f2 = jnp.einsum('bhnd,hd->bhn', support, weight_v[..., 0])[:, :, :, None]
        logits = f1 + f2
        w = jnp.where(logits >= 0, logits, NEG_SLOPE * logits)
        masked = jnp.einsum('bhik,bkj->bhij', w, adj)
        mask = masked != 0
        attn = jax.nn.softmax(jnp.where(mask, masked, -jnp.inf), axis=3)
        attn = jnp.where(mask, attn, 0.0)
        out = jnp.einsum('bhij,bhjd->bhid', attn, support)
        out = out.transpose(0, 2, 1, 3).reshape(b, n, H * D)
        out = out + bias + inputs @ proj_w.T + proj_b
        return jnp.tanh(out)

    def _L1_gnn_ref(x, mask, Wv, bv, Wk, bk, Wq, bq):
        import jax, jax.numpy as jnp
        import numpy as np
        B, N, DIN, HID = (8, 1024, 128, 128)
        CLAMP_HI = 90000000000000.0
        NEG_PENALTY = 9000000000000000.0
        v = jax.nn.relu(jnp.einsum('bnd,hd->bnh', x, Wv) + bv)
        q = jax.nn.relu(jnp.einsum('bnd,hd->bnh', x, Wq) + bq)
        k = jax.nn.relu(jnp.einsum('bnd,hd->bnh', x, Wk) + bk)
        scores = jnp.einsum('bih,bjh->bij', q, k)
        h = jnp.clip(scores * mask, 0.0, CLAMP_HI) - NEG_PENALTY * (1.0 - mask)
        att = jax.nn.softmax(h, axis=2)
        out = jnp.einsum('bij,bjh->bih', att, v)
        return out
    x = _layernorm(x + _L0_gnn_ref(x, adj, L0_gnn_weight, L0_gnn_weight_u, L0_gnn_weight_v, L0_gnn_bias, L0_gnn_proj_w, L0_gnn_proj_b), axis=-1)
    x = _layernorm(x + _L1_gnn_ref(x, adj, L1_gnn_Wv, L1_gnn_bv, L1_gnn_Wk, L1_gnn_bk, L1_gnn_Wq, L1_gnn_bq), axis=-1)
    return x

_drawn_inputs = setup_inputs


def setup_inputs(seed=0):
    import zlib

    import numpy as np

    out = dict(_drawn_inputs(seed))
    spreads = {}
    factors = {'L1_gnn_bk': 4.192, 'L1_gnn_bq': 3.362}
    for name, (base, spread) in spreads.items():
        noise = np.random.default_rng([zlib.crc32(name.encode()), seed]).standard_normal(out[name].shape)
        drawn = base * np.exp(spread * noise) if base else spread * noise
        out[name] = jnp.asarray(drawn.astype(out[name].dtype))
    for name, factor in factors.items():
        out[name] = (out[name] * factor).astype(out[name].dtype)
    return out
```

```python
from contextlib import ExitStack

import concourse.bass as bass
from concourse import mybir

F32 = mybir.dt.float32
F32R = mybir.dt.float32r
BF16 = mybir.dt.bfloat16
ALU = mybir.AluOpType
ACT = mybir.ActivationFunctionType
AX_X = mybir.AxisListType.X

GRAPHS, N, F = 16, 512, 128
H, D = 4, 32
P = 128
NB = N // P
SLOTS = 20
LAG_T, LAG_V = 2, 3
UNITS = {0: 0, 4: 1, 8: 2, 16: 3}
DENSE = 12
RING = 4

SLOPE = 0.2
ZERO_ROW = 1e-6
CLAMP_HI = 9e13
NEG_PENALTY = 9e15
BIG = 3e38
EPS = 1e-5
FOLD_STEPS = 6

NEXT_JOBS = {3: "f2", 4: "sp0", 5: "sp1", 11: "f1"}
PREV_JOBS = {7: "x1t", 8: "q", 9: "k", 10: "v", 15: "o0", 16: "o1", 17: "o2", 18: "o3"}


def side_jobs(has_prev, has_next):
    jobs = {}
    if has_next:
        jobs.update(NEXT_JOBS)
    if has_prev:
        jobs.update(PREV_JOBS)
    return dict(sorted(jobs.items()))


class Turn:

    def __init__(self, g, parity):
        self.g, self.p = g, parity
        fixed = isinstance(g, int)
        self.heads = not fixed or 0 <= g < GRAPHS
        self.prev = not fixed or g >= 1
        self.next = not fixed or g < GRAPHS - 1
        self.fixed = fixed
        jobs = side_jobs(self.prev, self.next)
        self.job = jobs
        order = {name: i for i, name in enumerate(jobs.values())}
        full = len(side_jobs(True, True))
        part = len(NEXT_JOBS)
        if fixed and g < 1:
            base = part * (g + 1)
        elif fixed and g == GRAPHS:
            base = 2 * part + full * (GRAPHS - 2) + len(PREV_JOBS)
        else:
            base = g * full + (2 * part - full)
        self.side = {name: base + i for name, i in order.items()}
        self.side_base = base

    def has_tile(self, s):
        if s < 0:
            return self.prev
        dense = DENSE <= s < DENSE + NB
        return self.prev if dense else self.heads

    def tile(self, s):
        if self.fixed and self.g == 0:
            return s if s < DENSE else s - NB
        if self.fixed and self.g == GRAPHS:
            return (SLOTS * GRAPHS - NB) + (s if s <= 0 else s - DENSE)
        return self.g * SLOTS + (s - NB)

    def head_tile(self, s):
        return self.g * (H * NB) + (s if s < DENSE else s - NB)

    def slot_ring_back(self, s):
        if self.fixed and self.g == 0 and s >= DENSE:
            return s - 2 * RING
        if self.fixed and self.g == GRAPHS and s >= DENSE:
            return s - DENSE - RING
        return s - RING

    def unit(self, h):
        return self.g * H + h


def turns(eng):
    for g in (-1, 0, 1):
        yield Turn(g, g % 2)
    with eng.Fori(0, (GRAPHS - 4) // 2) as step:
        yield Turn(step * 2 + 2, 0)
        yield Turn(step * 2 + 3, 1)
    for g in (GRAPHS - 2, GRAPHS - 1, GRAPHS):
        yield Turn(g, g % 2)


def due(count):
    return not isinstance(count, int) or count > 0


def build(nc, x, xT, adj, w0, u0, v0, bias0, projT, proj_b, wvT, bv, wkT, bk, wqT, bq, out):
    with ExitStack() as ctx:
        def sb(name, shape, dt=F32):
            return ctx.enter_context(nc.sbuf_tensor(name, shape, dt))

        def ps(name, shape, dt=F32):
            return ctx.enter_context(nc.psum_tensor(name, shape, dt))

        def sem(name):
            return ctx.enter_context(nc.semaphore(name))

        f2_dram = nc.dram_tensor("f2_rows", [2, H, N], F32, kind="Internal").ap()

        ident = sb("ident", [P, P])
        wp = sb("wp", [P, 2 * P])
        uv_row = sb("uv_row", [P, 2, P])
        wuv = sb("wuv", [P, 2, P])
        w_f1 = sb("w_f1", [P, H])
        w_f2 = sb("w_f2", [P, H])
        bias_rows = sb("bias_rows", [P, 2, P])
        bias_row = sb("bias_row", [P, P])
        wv_sb = sb("wv_sb", [P, P])
        wk_sb = sb("wk_sb", [P, P])
        wq_sb = sb("wq_sb", [P, P])
        bv_row = sb("bv_row", [P, P])
        bq_col = sb("bq_col", [P, 1])
        bk_col = sb("bk_col", [P, 1])
        half = sb("half", [P, NB])

        x_sb = [sb(f"x_sb{i}", [P, NB, F]) for i in range(2)]
        xT_sb = sb("xT_sb", [P, N])
        adj_sb = [sb(f"adj_sb{i}", [P, NB, N]) for i in range(2)]
        adj_r = [sb(f"adj_r{i}", [P, NB, N], F32R) for i in range(2)]
        cap = sb("cap", [P, NB, N])
        rowsum = sb("rowsum", [P, NB])
        row_zero = sb("row_zero", [P, NB])
        row_scale = [sb(f"row_scale{i}", [P, NB]) for i in range(2)]
        f1 = [sb(f"f1_{i}", [P, NB, H]) for i in range(2)]
        f2_row = sb("f2_row", [H, N])
        f2_all = [sb(f"f2_all{i}", [P, H, N]) for i in range(2)]
        support = [sb(f"support{i}", [P, NB, P]) for i in range(2)]
        skip = [sb(f"skip{i}", [P, NB, P]) for i in range(2)]
        neg_max = [sb(f"neg_max{i}", [P, NB, H]) for i in range(2)]
        sums = [sb(f"sums{i}", [P, NB, H]) for i in range(2)]

        w = [sb(f"w{i}", [P, NB, N]) for i in range(2)]
        w_hi = [sb(f"w_hi{i}", [P, NB, N], F32R) for i in range(2)]
        w_lo = [sb(f"w_lo{i}", [P, NB, N], F32R) for i in range(2)]

        zero_pen = [sb(f"zero_pen{i}", [P, N], BF16) for i in range(2)]
        neg_h = [sb(f"neg_h{i}", [P, N]) for i in range(RING)]
        prob = [sb(f"prob{i}", [P, N]) for i in range(RING)]
        probT = [sb(f"probT{i}", [P, N]) for i in range(RING)]
        scrap = sb("scrap", [P, N], BF16)

        recip = sb("recip", [P, NB, H])
        head_scale = sb("head_scale", [P, NB, H])
        att = sb("att", [P, NB, P])
        pre = sb("pre", [P, NB, P])
        th = sb("th", [P, NB, P])
        y = sb("y", [P, NB, P])
        stats = sb("stats", [P, NB, 6])
        mean_var = sb("mean_var", [P, NB, 2])
        var_eps = sb("var_eps", [P, NB])
        rstd = sb("rstd", [P, NB])
        x1 = sb("x1", [P, NB, P])
        x1T = sb("x1T", [P, N])
        qT = sb("qT", [P, N])
        kT = sb("kT", [P, N])
        v_pre = sb("v_pre", [P, NB, P])
        v_sb = sb("v_sb", [P, NB, P])
        d_max = sb("d_max", [P, NB])
        d_neg_max = sb("d_neg_max", [P, NB])
        d_sums = sb("d_sums", [P, NB])
        d_recip = sb("d_recip", [P, NB])
        y2 = sb("y2", [P, NB, P])
        stats2 = sb("stats2", [P, NB, 6])
        mean_var2 = sb("mean_var2", [P, NB, 2])
        var_eps2 = sb("var_eps2", [P, NB])
        rstd2 = sb("rstd2", [P, NB])
        out_sb = sb("out_sb", [P, NB, P])

        score = [ps(f"score{i}", [P, N]) for i in range(RING)]
        flip = [ps(f"flip{i}", [P, N]) for i in range(2)]
        head_out = ps("head_out", [P, NB, P])
        side = ps("side", [P, N])

        s_weights = sem("weights_loaded")
        s_x = [sem(f"x_loaded{i}") for i in range(2)]
        s_xT = sem("xT_loaded")
        s_adj = [sem(f"adj_loaded{i}") for i in range(2)]
        s_f2_stored = sem("f2_stored")
        s_f2_all = [sem(f"f2_all_loaded{i}") for i in range(2)]
        s_stored = sem("out_stored")
        s_ident = sem("ident_ready")
        s_fold = sem("folded_weights_steps")
        s_score = sem("score_done")
        s_flip = sem("flip_done")
        s_value = sem("value_done")
        s_side = sem("side_done")
        s_side_read = sem("side_read")
        s_pen = sem("zero_pen_ready")
        s_masked = sem("masked_ready")
        s_dmax = sem("dense_max_steps")
        s_exp = sem("exp_done")
        s_probT = sem("probT_ready")
        s_logit = sem("logit_ready")
        s_lrelu = sem("lrelu_done")
        s_hi = sem("w_hi_ready")
        s_lo_a = sem("w_lo_a_ready")
        s_lo_b = sem("w_lo_b_ready")
        s_rowsum = sem("rowsum_ready")
        s_rows = sem("row_scale_ready")
        s_adj_r = sem("adj_r_ready")
        s_cap = sem("cap_ready")
        s_recip = sem("recip_steps")
        s_att = sem("att_ready")
        s_pre = sem("pre_ready")
        s_tanh = sem("tanh_done")
        s_y = sem("y_ready")
        s_stats = sem("stats_steps")
        s_eps = sem("var_eps_ready")
        s_rstd = sem("rstd_ready")
        s_x1 = sem("x1_ready")
        s_v = sem("v_ready")
        s_dinv = sem("dense_recip_ready")
        s_stats2 = sem("stats2_steps")
        s_y2 = sem("y2_ready")
        s_eps2 = sem("var_eps2_ready")
        s_rstd2 = sem("rstd2_ready")
        s_out = sem("out_ready")

        WEIGHT_LOADS = 12
        weights_loaded = 16 * WEIGHT_LOADS

        def loads(graph, parity):
            return (graph - parity) * 8 + 16

        def rows(dram, graph):
            return dram[bass.ds(graph, 1)].rearrange("o (b p) f -> p (o b) f", p=P)

        block = ctx.enter_context(nc.Block())

        @block.sync
        def _(sp):
            def load(dst, src):
                sp.dma_start(dst, src).then_inc(s_weights, 16)

            load(wp[:, 0:P], w0)
            load(wp[:, P:2 * P], projT)
            load(uv_row[:, 0, :], u0.broadcast_to([P, P]))
            load(uv_row[:, 1, :], v0.broadcast_to([P, P]))
            load(bias_rows[:, 0, :], bias0.broadcast_to([P, P]))
            load(bias_rows[:, 1, :], proj_b.broadcast_to([P, P]))
            load(wv_sb[:], wvT)
            load(wk_sb[:], wkT)
            load(wq_sb[:], wqT)
            load(bv_row[:], bv.broadcast_to([P, P]))
            load(bq_col[:], bq)
            load(bk_col[:], bk)

            for t in turns(sp):
                g, q = t.g, 1 - t.p
                if t.next:
                    if due(t.side_base):
                        sp.wait_ge(s_side, t.side_base)
                        sp.nop(nofuse=True)
                    sp.dma_start(xT_sb[:], xT[bass.ds(g + 1, 1)].rearrange("o f n -> (o f) n")).then_inc(s_xT, 16)
                    if t.prev:
                        sp.wait_ge(s_cap, g)
                        sp.nop(nofuse=True)
                    sp.dma_start(adj_sb[q][:], rows(adj, g + 1)).then_inc(s_adj[q], 16)
                    sp.wait_ge(s_side_read, t.side["f2"] + 1)
                    sp.nop(nofuse=True)
                    sp.dma_start(f2_dram[q], f2_row[:]).then_inc(s_f2_stored, 16)
                    sp.wait_ge(s_f2_stored, (g + 2) * 16)
                    sp.nop(nofuse=True)
                    if t.prev:
                        sp.wait_ge(s_logit, g * H)
                        sp.nop(nofuse=True)
                    sp.dma_start(f2_all[q][:], f2_dram[q:q + 1].broadcast_to([P, H, N])).then_inc(s_f2_all[q], 16)
                    if t.prev:
                        sp.wait_ge(s_y, g)
                        sp.nop(nofuse=True)
                    sp.dma_start(x_sb[q][:], rows(x, g + 1)).then_inc(s_x[q], 16)
                if t.prev:
                    sp.wait_ge(s_out, g)
                    sp.nop(nofuse=True)
                    sp.dma_start(rows(out, g - 1), out_sb[:]).then_inc(s_stored, 16)
            sp.wait_ge(s_stored, 16 * GRAPHS)

        @block.tensor
        def _(pe):
            def head_scores(t, s, h, i):
                n, k = t.tile(s), h % 2
                if i == 0:
                    pe.wait_ge(s_hi, 2 * (t.unit(h) + 1))
                    pe.wait_ge(s_lo_a, t.unit(h) + 1)
                    pe.wait_ge(s_lo_b, t.unit(h) + 1)
                    if h == 0:
                        pe.wait_ge(s_adj_r, t.g + 1)
                if due(n - RING + 1):
                    pe.wait_ge(s_masked, n - RING + 1)
                for part in (w_hi[k], w_lo[k]):
                    for b in range(NB):
                        mm = nc.tensor.matmul(score[s % RING][:], part[:, b, i * P:(i + 1) * P], adj_r[t.p][:, b, :],
                                              start=(part is w_hi[k] and b == 0),
                                              stop=(part is w_lo[k] and b == NB - 1))
                mm.then_inc(s_score, 1)

            def dense_scores(t, s, i):
                pe.wait_ge(s_side_read, t.side["k"] + 1)
                pe.wait_ge(s_masked, t.tile(s) - RING + 1)
                nc.tensor.matmul(score[s % RING][:], qT[:, i * P:(i + 1) * P], kT[:],
                                 start=True, stop=True).then_inc(s_score, 1)

            def flip_tile(t, s):
                n = t.tile(s)
                pe.wait_ge(s_exp, n + 1)
                if due(n - 1):
                    pe.wait_ge(s_probT, n - 1)
                for b in range(NB):
                    mm = nc.tensor.transpose(flip[s % 2][:, b * P:(b + 1) * P], prob[s % RING][:, b * P:(b + 1) * P],
                                             ident[:])
                mm.then_inc(s_flip, 1)

            def head_values(t, s):
                h, i = (3, s + NB) if s < 0 else (UNITS[s - s % NB], s % NB)
                p = 1 - t.p if s < 0 else t.p
                pe.wait_ge(s_probT, t.tile(s) + 1)
                if s == 0:
                    if due(t.g):
                        pe.wait_ge(s_att, t.g)
                for b in range(NB):
                    mm = nc.tensor.matmul(head_out[:, i, h * D:(h + 1) * D], probT[s % RING][:, b * P:(b + 1) * P],
                                          support[p][:, b, h * D:(h + 1) * D], start=(b == 0), stop=(b == NB - 1))
                mm.then_inc(s_value, 1)

            def side_job(t, s):
                name = t.job[s]
                if name in ("f2", "sp0", "sp1", "f1"):
                    pe.wait_ge(s_xT, (t.g + 2) * 16)
                if name == "x1t":
                    pe.wait_ge(s_x1, t.g)
                if name[0] == "o":
                    pe.wait_ge(s_probT, t.tile(DENSE + int(name[1])) + 1)
                    pe.wait_ge(s_v, t.g)
                if due(t.side[name]):
                    pe.wait_ge(s_side_read, t.side[name])
                if name == "f2":
                    mm = nc.tensor.matmul(side[0:H, :], w_f2[:], xT_sb[:], start=True, stop=True)
                elif name in ("sp0", "sp1"):
                    for b in range(2):
                        at = (2 * int(name[2]) + b) * P
                        mm = nc.tensor.matmul(side[:, b * 2 * P:(b + 1) * 2 * P], xT_sb[:, at:at + P], wp[:],
                                              start=True, stop=True)
                elif name == "f1":
                    for b in range(NB):
                        mm = nc.tensor.matmul(side[:, b * H:(b + 1) * H], xT_sb[:, b * P:(b + 1) * P], w_f1[:],
                                              start=True, stop=True)
                elif name == "x1t":
                    for b in range(NB):
                        mm = nc.tensor.transpose(side[:, b * P:(b + 1) * P], x1[:, b, :], ident[:])
                elif name in ("q", "k"):
                    mm = nc.tensor.matmul(side[:], (wq_sb if name == "q" else wk_sb)[:], x1T[:], start=True, stop=True)
                elif name == "v":
                    for b in range(NB):
                        mm = nc.tensor.matmul(side[:, b * P:(b + 1) * P], x1T[:, b * P:(b + 1) * P], wv_sb[:],
                                              start=True, stop=True)
                else:
                    i = int(name[1])
                    for b in range(NB):
                        mm = nc.tensor.matmul(side[:, 0:P], probT[i % RING][:, b * P:(b + 1) * P], v_sb[:, b, :],
                                              start=(b == 0), stop=(b == NB - 1))
                mm.then_inc(s_side, 1)

            pe.wait_ge(s_ident, 2)
            pe.wait_ge(s_weights, weights_loaded)
            pe.wait_ge(s_fold, FOLD_STEPS)
            for t in turns(pe):
                for s in range(SLOTS):
                    if t.has_tile(s):
                        if DENSE <= s < DENSE + NB:
                            dense_scores(t, s, s - DENSE)
                        else:
                            head_scores(t, s, UNITS[s - s % NB], s % NB)
                    if s in t.job and t.job[s][0] != "o":
                        side_job(t, s)
                    if t.has_tile(s - LAG_T):
                        flip_tile(t, s - LAG_T)
                    if s in t.job and t.job[s][0] == "o":
                        side_job(t, s)
                    elif t.has_tile(s - LAG_V):
                        head_values(t, s - LAG_V)

        @block.scalar
        def _(act):
            def side_out(t, name):
                act.wait_ge(s_side, t.side[name] + 1)
                if name == "f2":
                    if due((t.g + 1) * 16):
                        act.wait_ge(s_f2_stored, (t.g + 1) * 16)
                    op = nc.scalar.copy(f2_row[:], side[0:H, :])
                elif name == "x1t":
                    op = nc.scalar.copy(x1T[:], side[:])
                elif name == "q":
                    op = nc.scalar.activation(qT[:], side[:], ACT.Relu, bias=bq_col[:, 0:1])
                else:
                    op = nc.scalar.activation(kT[:], side[:], ACT.Relu, bias=bk_col[:, 0:1])
                op.then_inc(s_side_read, 1)

            def exp_tile(t, s):
                n = t.tile(s)
                act.wait_ge(s_masked, n + 1)
                if due(n - RING + 1):
                    act.wait_ge(s_flip, n - RING + 1)
                if DENSE <= s < DENSE + NB:
                    i = s - DENSE
                    op = nc.scalar.activation(prob[s % RING][:], neg_h[s % RING][:], ACT.Exp,
                                              bias=d_neg_max[:, i:i + 1], accum_out=d_sums[:, i:i + 1])
                else:
                    h, i = UNITS[s - s % NB], s % NB
                    op = nc.scalar.activation(prob[s % RING][:], neg_h[s % RING][:], ACT.Exp, scale=-1.0,
                                              bias=neg_max[t.p][:, i, h:h + 1], accum_out=sums[t.p][:, i, h:h + 1])
                op.then_inc(s_exp, 1)

            def copy_flipped(t, s):
                act.wait_ge(s_flip, t.tile(s) + 1)
                back = t.slot_ring_back(s)
                if back < -NB:
                    act.wait_ge(s_side, t.side_base)
                    act.wait_ge(s_value, t.head_tile(-NB))
                elif DENSE <= back < DENSE + NB:
                    act.wait_ge(s_side, t.side[f"o{back - DENSE}"] + 1)
                else:
                    if due(t.head_tile(back) + 1):
                        act.wait_ge(s_value, t.head_tile(back) + 1)
                nc.scalar.copy(probT[s % RING][:], flip[s % 2][:]).then_inc(s_probT, 1)

            def logits(t, graph, p, h, b):
                u = graph * H + h
                if b == 0:
                    if due(u - 1):
                        act.wait_ge(s_lo_a, u - 1)
                        act.wait_ge(s_lo_b, u - 1)
                    if h == 0:
                        act.wait_ge(s_f2_all[p], loads(graph, p))
                        act.wait_ge(s_side_read, t.side["f1"] + 1)
                op = nc.scalar.activation(w[h % 2][:, b, :], f2_all[p][:, h, :], ACT.Identity,
                                          scale=row_scale[p][:, b:b + 1], bias=f1[p][:, b, h:h + 1])
                if b == NB - 1:
                    op.then_inc(s_logit, 1)

            act.wait_ge(s_weights, weights_loaded)
            for t in turns(act):
                g, q = t.g, 1 - t.p
                for s in range(SLOTS):
                    b = s % NB
                    if s < 4 and t.heads:
                        logits(t, g, t.p, 2, b)
                    if 8 <= s < 12 and t.heads:
                        logits(t, g, t.p, 3, b)
                    if 12 <= s < 16 and t.next:
                        logits(t, g + 1, q, 0, b)
                    if 16 <= s and t.next:
                        logits(t, g + 1, q, 1, b)
                    if t.job.get(s) in ("f2", "x1t", "q", "k"):
                        side_out(t, t.job[s])
                    if t.has_tile(s):
                        exp_tile(t, s)
                    if t.has_tile(s - 1):
                        copy_flipped(t, s - 1)
                    if 4 <= s < 8 and t.next:
                        if b == 0:
                            act.wait_ge(s_adj[q], loads(g + 1, q))
                            if due(2 * (g + 1)):
                                act.wait_ge(s_rows, 2 * (g + 1))
                        if due(NB * (g + 1) + b):
                            act.wait_ge(s_rowsum, NB * (g + 1) + b)
                        nc.scalar.activation(scrap[:], adj_sb[q][:, b, :], ACT.Identity,
                                             accum_out=rowsum[:, b:b + 1]).then_inc(s_rowsum, 1)
                    if s == 3 and t.prev:
                        act.wait_ge(s_pre, g)
                        nc.scalar.activation(th[:], pre[:], ACT.Tanh).then_inc(s_tanh, 1)

        @block.vector
        def _(dve):
            def mask_head(t, s):
                n, m, h, i = t.tile(s), t.head_tile(s), UNITS[s - s % NB], s % NB
                dve.wait_ge(s_score, n + 1)
                if due(n - 1):
                    dve.wait_ge(s_masked, n - 1)
                nc.vector.tensor_scalar(zero_pen[s % 2][:], score[s % RING][:], 0.0, -BIG, ALU.is_equal,
                                        ALU.mult).then_inc(s_pen, 1)
                if due(n - RING + 1):
                    dve.wait_ge(s_exp, n - RING + 1)
                dve.wait_ge(s_pen, m + 1)
                dve.nop(nofuse=True)
                nc.vector.tensor_tensor_reduce(neg_h[s % RING][:], score[s % RING][:], zero_pen[s % 2][:], -1.0, BIG,
                                               ALU.add, ALU.min, neg_max[t.p][:, i, h:h + 1]).then_inc(s_masked, 1)

            def mask_dense(t, s):
                n, i = t.tile(s), s - DENSE
                step = 2 * (NB * (t.g - 1) + i)
                dve.wait_ge(s_score, n + 1)
                dve.wait_ge(s_exp, n - RING + 1)
                if i == 0:
                    dve.wait_ge(s_cap, t.g)
                nc.vector.scalar_tensor_tensor(out=neg_h[s % RING][:], in0=score[s % RING][:], scalar=CLAMP_HI,
                                               in1=cap[:, i, :], op0=ALU.min, op1=ALU.min).then_inc(s_dmax, 1)
                dve.wait_ge(s_dmax, step + 1)
                nc.vector.tensor_reduce(d_max[:, i:i + 1], neg_h[s % RING][:], AX_X, ALU.max).then_inc(s_dmax, 1)
                dve.wait_ge(s_dmax, step + 2)
                nc.vector.tensor_scalar(d_neg_max[:, i:i + 1], d_max[:, i:i + 1], -1.0, None,
                                        ALU.mult).then_inc(s_masked, 1)

            def split_half(unit, h, half, free):
                part = slice(half * NB // 2, (half + 1) * NB // 2)
                if half == 0:
                    dve.wait_ge(s_logit, unit + 1)
                nc.vector.scalar_tensor_tensor(out=w[h % 2][:, part, :], in0=w[h % 2][:, part, :], scalar=SLOPE,
                                               in1=w[h % 2][:, part, :], op0=ALU.mult, op1=ALU.max)\
                    .then_inc(s_lrelu, 1)
                if due(free):
                    dve.wait_ge(s_score, free)
                dve.wait_ge(s_lrelu, 2 * unit + half + 1)
                nc.vector.tensor_copy(w_hi[h % 2][:, part, :], w[h % 2][:, part, :]).then_inc(s_hi, 1)
                if half == 1:
                    dve.wait_ge(s_hi, 2 * unit + 2)
                    nc.vector.tensor_tensor(w_lo[h % 2][:, part, :], w[h % 2][:, part, :],
                                            w_hi[h % 2][:, part, :].bitcast(F32), ALU.subtract).then_inc(s_lo_b, 1)

            def split_at(t, s, half):
                if s == 0 and t.heads:
                    split_half(t.unit(1), 1, half, t.tile(0))
                if s == 4 and t.heads:
                    split_half(t.unit(2), 2, half, t.tile(3) + 1)
                if s == 12 and t.heads:
                    split_half(t.unit(3), 3, half, t.tile(7) + 1)
                if s == 16 and t.next:
                    split_half(t.unit(H), 0, half, t.tile(11) + 1 if t.heads else 0)

            def normalise_heads(t):
                g, o = t.g, 1 - t.p
                dve.wait_ge(s_exp, t.tile(0))
                if due(g - 1):
                    dve.wait_ge(s_att, g - 1)
                nc.vector.reciprocal(recip[:], sums[o][:]).then_inc(s_recip, 1)
                dve.wait_ge(s_recip, 2 * g - 1)
                nc.vector.scalar_tensor_tensor(out=head_scale[:], in0=neg_max[o][:], scalar=0.5 * BIG, in1=recip[:],
                                               op0=ALU.is_lt, op1=ALU.mult).then_inc(s_recip, 1)
                dve.wait_ge(s_recip, 2 * g)
                dve.wait_ge(s_value, g * (H * NB))
                if due(g - 1):
                    dve.wait_ge(s_pre, g - 1)
                nc.vector.tensor_tensor(att[:].rearrange("p b (h d) -> p (b h) d", h=H),
                                        head_out[:].rearrange("p b (h d) -> p (b h) d", h=H),
                                        head_scale[:].rearrange("p b (h o) -> p (b h) o", o=1)
                                        .broadcast_to([P, NB * H, D]), ALU.mult).then_inc(s_att, 1)

            def row_stats(src, into, total, s_steps, g):
                for b in range(NB):
                    op = nc.vector.bn_stats(into[:, b, :], src[:, b, :])
                op.then_inc(s_steps, 1)
                dve.wait_ge(s_steps, 2 * g - 1)
                dve.nop(nofuse=True)
                for b in range(NB):
                    op = nc.vector.bn_aggr(total[:, b, :], into[:, b, :])
                op.then_inc(s_steps, 1)

            def centre_scale(dst, src, total, scale, done):
                for b in range(NB):
                    op = nc.vector.tensor_scalar(dst[:, b, :], src[:, b, :], total[:, b, 0:1], scale[:, b:b + 1],
                                                 ALU.subtract, ALU.mult)
                op.then_inc(done, 1)

            def side_out(t, name):
                q = 1 - t.p
                dve.wait_ge(s_side, t.side[name] + 1)
                if name in ("sp0", "sp1"):
                    at = 2 * int(name[2])
                    both = side[:].rearrange("p (b n) -> p b n", b=2)
                    if t.prev:
                        dve.wait_ge(s_pre, t.g)
                    nc.vector.tensor_copy(support[q][:, at:at + 2, :], both[:, :, 0:P])
                    nc.vector.tensor_tensor(skip[q][:, at:at + 2, :], both[:, :, P:2 * P],
                                            bias_row[:].rearrange("p (o n) -> p o n", o=1).broadcast_to([P, 2, P]),
                                            ALU.add).then_inc(s_side_read, 1)
                elif name == "f1":
                    if t.prev:
                        dve.wait_ge(s_logit, t.g * H)
                    dve.wait_ge(s_rows, 2 * (t.g + 2))
                    nc.vector.tensor_tensor(f1[q][:], side[:, 0:NB * H].rearrange("p (b h) -> p b h", b=NB),
                                            row_scale[q][:].rearrange("p (b o) -> p b o", o=1)
                                            .broadcast_to([P, NB, H]), ALU.mult).then_inc(s_side_read, 1)
                elif name == "v":
                    if due(t.g - 1):
                        dve.wait_ge(s_v, t.g - 1)
                    nc.vector.tensor_tensor(v_pre[:], side[:].rearrange("p (b n) -> p b n", b=NB),
                                            bv_row[:].rearrange("p (o n) -> p o n", o=1).broadcast_to([P, NB, P]),
                                            ALU.add).then_inc(s_side_read, 1)
                else:
                    i = int(name[1])
                    if i == 0:
                        if due(t.g - 1):
                            dve.wait_ge(s_out, t.g - 1)
                    nc.vector.reciprocal(d_recip[:, i:i + 1], d_sums[:, i:i + 1]).then_inc(s_dinv, 1)
                    dve.wait_ge(s_dinv, NB * (t.g - 1) + i + 1)
                    nc.vector.scalar_tensor_tensor(out=y2[:, i, :], in0=side[:, 0:P], scalar=d_recip[:, i:i + 1],
                                                   in1=x1[:, i, :], op0=ALU.mult, op1=ALU.add)\
                        .then_inc(s_side_read, 1)

            dve.wait_ge(s_weights, weights_loaded)
            nc.vector.memset(half[:], -0.5).then_inc(s_fold, 1)
            nc.vector.tensor_tensor(bias_row[:], bias_rows[:, 0, :], bias_rows[:, 1, :], ALU.add).then_inc(s_fold, 1)
            for k in range(2):
                nc.vector.tensor_tensor(wuv[:, k, :], wp[:, 0:P], uv_row[:, k, :], ALU.mult).then_inc(s_fold, 1)
            dve.wait_ge(s_fold, 4)
            for k, folded in enumerate((w_f1, w_f2)):
                nc.vector.tensor_reduce(folded[:], wuv[:, k, :].rearrange("p (h d) -> p h d", h=H), AX_X,
                                        ALU.add).then_inc(s_fold, 1)

            for t in turns(dve):
                g, q = t.g, 1 - t.p
                for s in range(SLOTS):
                    split_at(t, s, 0)
                    if t.has_tile(s):
                        (mask_dense if DENSE <= s < DENSE + NB else mask_head)(t, s)
                    split_at(t, s, 1)
                    if t.job.get(s, "q") not in ("f2", "x1t", "q", "k"):
                        side_out(t, t.job[s])
                    if s == 2 and t.prev:
                        normalise_heads(t)
                    if s == 5 and t.prev:
                        dve.wait_ge(s_y, g)
                        if due(g - 1):
                            dve.wait_ge(s_x1, g - 1)
                        row_stats(y, stats, mean_var, s_stats, g)
                    if s == 6 and t.prev:
                        dve.wait_ge(s_rstd, g)
                        dve.wait_ge(s_side_read, t.side_base)
                        centre_scale(x1, y, mean_var, rstd, s_x1)
                    if s == 10 and t.next:
                        dve.wait_ge(s_rowsum, NB * (g + 2))
                        if due(g + 1):
                            dve.wait_ge(s_adj_r, g + 1)
                        nc.vector.tensor_scalar(row_zero[:], rowsum[:], 0.0, None, ALU.is_equal).then_inc(s_rows, 1)
                        if t.prev:
                            dve.wait_ge(s_logit, g * H)
                        nc.vector.tensor_scalar(row_scale[q][:], rowsum[:], 0.0, ZERO_ROW, ALU.is_gt,
                                                ALU.max).then_inc(s_rows, 1)
                    if s == 18 and t.prev:
                        dve.wait_ge(s_side_read, t.side["o3"] + 1)
                        row_stats(y2, stats2, mean_var2, s_stats2, g)
                    if s == 19 and t.prev:
                        dve.wait_ge(s_rstd2, g)
                        if due(16 * (g - 1)):
                            dve.wait_ge(s_stored, 16 * (g - 1))
                        centre_scale(out_sb, y2, mean_var2, rstd2, s_out)

        @block.gpsimd
        def _(pool):
            def split_lo(unit, h):
                part = slice(0, NB // 2)
                pool.wait_ge(s_hi, 2 * unit + 1)
                nc.gpsimd.tensor_tensor(w_lo[h % 2][:, part, :], w[h % 2][:, part, :],
                                        w_hi[h % 2][:, part, :].bitcast(F32), ALU.subtract).then_inc(s_lo_a, 1)

            def inverse_std(total, shifted, scale, s_steps, s_shift, done, g):
                pool.wait_ge(s_steps, 2 * g)
                pool.nop(nofuse=True)
                nc.gpsimd.tensor_scalar(shifted[:], total[:, :, 1], EPS, None, ALU.add).then_inc(s_shift, 1)
                pool.wait_ge(s_shift, g)
                nc.gpsimd.tensor_tensor(scale[:], shifted[:], half[:], ALU.pow).then_inc(done, 1)

            nc.gpsimd.memset(ident[:], 0.0).then_inc(s_ident, 1)
            pool.wait_ge(s_ident, 1)
            nc.gpsimd.affine_select(out=ident[:], in_=ident[:], compare_op=ALU.not_equal, fill=1.0, base=0,
                                    pattern=[[-1, P]], channel_multiplier=1).then_inc(s_ident, 1)
            pool.wait_ge(s_fold, FOLD_STEPS)

            for t in turns(pool):
                g, q = t.g, 1 - t.p
                if t.heads:
                    split_lo(t.unit(1), 1)
                if t.prev:
                    pool.wait_ge(s_att, g)
                    if due(g - 1):
                        pool.wait_ge(s_tanh, g - 1)
                    nc.gpsimd.tensor_tensor(pre[:], att[:], skip[q][:], ALU.add).then_inc(s_pre, 1)
                    pool.wait_ge(s_tanh, g)
                    pool.wait_ge(s_x[q], loads(g - 1, q))
                    if due(g - 1):
                        pool.wait_ge(s_x1, g - 1)
                    nc.gpsimd.tensor_tensor(y[:], x_sb[q][:], th[:], ALU.add).then_inc(s_y, 1)
                if t.heads:
                    split_lo(t.unit(2), 2)
                if t.prev:
                    inverse_std(mean_var, var_eps, rstd, s_stats, s_eps, s_rstd, g)
                if t.prev:
                    pool.wait_ge(s_side_read, t.side["v"] + 1)
                    if not t.fixed or g > 1:
                        pool.wait_ge(s_side, t.side_base)
                        pool.nop(nofuse=True)
                    nc.gpsimd.tensor_scalar(v_sb[:], v_pre[:], 0.0, None, ALU.max).then_inc(s_v, 1)
                if t.next:
                    pool.wait_ge(s_rows, 2 * (g + 2))
                    if t.prev:
                        pool.wait_ge(s_score, t.tile(0))
                        pool.nop(nofuse=True)
                    for b in range(NB):
                        op = nc.gpsimd.tensor_scalar(adj_r[q][:, b, :], adj_sb[q][:, b, :], 1.0,
                                                     row_zero[:, b:b + 1], ALU.mult, ALU.add)
                    op.then_inc(s_adj_r, 1)
                if t.heads:
                    split_lo(t.unit(3), 3)
                    pool.wait_ge(s_adj[t.p], loads(g, t.p))
                    if t.prev:
                        pool.wait_ge(s_masked, t.tile(DENSE + NB - 1) + 1)
                        pool.nop(nofuse=True)
                    nc.gpsimd.tensor_scalar(cap[:], adj_sb[t.p][:], 2 * NEG_PENALTY, -NEG_PENALTY, ALU.mult,
                                            ALU.add).then_inc(s_cap, 1)
                if t.next:
                    split_lo(t.unit(H), 0)
                if t.prev:
                    inverse_std(mean_var2, var_eps2, rstd2, s_stats2, s_eps2, s_rstd2, g)


def kernel(x, adj, L0_gnn_weight, L0_gnn_weight_u, L0_gnn_weight_v, L0_gnn_bias, L0_gnn_proj_w, L0_gnn_proj_b,
           L1_gnn_Wv, L1_gnn_bv, L1_gnn_Wk, L1_gnn_bk, L1_gnn_Wq, L1_gnn_bq):
    import numpy as np
    import concourse.bacc as bacc
    from concourse.bass_utils import run_bass_kernel_spmd

    def as_laid(a):
        return np.ascontiguousarray(np.asarray(a))

    arrays = {
        "x": as_laid(x),
        "xT": as_laid(np.asarray(x).transpose(0, 2, 1)),
        "adj": as_laid(adj),
        "w0": as_laid(L0_gnn_weight),
        "u0": as_laid(np.asarray(L0_gnn_weight_u).reshape(1, P)),
        "v0": as_laid(np.asarray(L0_gnn_weight_v).reshape(1, P)),
        "bias0": as_laid(np.asarray(L0_gnn_bias).reshape(1, P)),
        "projT": as_laid(np.asarray(L0_gnn_proj_w).T),
        "proj_b": as_laid(np.asarray(L0_gnn_proj_b).reshape(1, P)),
        "wvT": as_laid(np.asarray(L1_gnn_Wv).T),
        "bv": as_laid(np.asarray(L1_gnn_bv).reshape(1, P)),
        "wkT": as_laid(np.asarray(L1_gnn_Wk).T),
        "bk": as_laid(np.asarray(L1_gnn_bk).reshape(P, 1)),
        "wqT": as_laid(np.asarray(L1_gnn_Wq).T),
        "bq": as_laid(np.asarray(L1_gnn_bq).reshape(P, 1)),
    }
    nc = bacc.Bacc("TRN2", target_bir_lowering=False, num_devices=1)
    aps = {k: nc.dram_tensor(f"in_{k}", a.shape, mybir.dt.from_np(a.dtype), kind="ExternalInput").ap()
           for k, a in arrays.items()}
    out = nc.dram_tensor("out", (GRAPHS, N, F), F32, kind="ExternalOutput").ap()
    build(nc, **aps, out=out)
    result = run_bass_kernel_spmd(nc, [{f"in_{k}": a for k, a in arrays.items()}], core_ids=[0])
    return result.results[0]["out"]
```

```python
from contextlib import ExitStack

import concourse.bass as bass
from concourse import mybir

F32 = mybir.dt.float32
F32R = mybir.dt.float32r
BF16 = mybir.dt.bfloat16
ALU = mybir.AluOpType
ACT = mybir.ActivationFunctionType
AX_X = mybir.AxisListType.X

GRAPHS, N, F = 16, 512, 128
H, D = 4, 32
P = 128
NB = N // P
SLOTS = 20
LAG_T = {"head": 3, "dense": 3}
LAG_C = {k: v - 1 for k, v in LAG_T.items()}
LAG_V = {k: v + 1 for k, v in LAG_T.items()}
UNITS = {0: 0, 4: 1, 8: 2, 16: 3}
DENSE = 12
RING = 4

HALVES = 2

LOGITS = {0: ((2, 0), (2, 1)), 1: ((2, 2), (2, 3)), 6: ((3, 0), (3, 1)), 7: ((3, 2),), 8: ((3, 3),),
          9: ((H, 0),), 10: ((H, 1),), 11: ((H, 2),), 14: ((H, 3),),
          16: ((H + 1, 0),), 17: ((H + 1, 1),), 18: ((H + 1, 2),), 19: ((H + 1, 3),)}
LEAKY = {0: ((1, 3),), 1: ((2, 0),), 2: ((2, 1),), 3: ((2, 2),), 5: ((2, 3),), 7: ((3, 0),), 9: ((3, 1), (3, 2)),
         10: ((3, 3),), 11: ((H, 0),), 12: ((H, 1),), 13: ((H, 2),), 16: ((H, 3),),
         17: ((H + 1, 0),), 18: ((H + 1, 1),), 19: ((H + 1, 2),)}
ROUND = {0: (1, 0), 1: (1, 1), 4: (2, 0), 5: (2, 1), 10: (3, 0), 11: (3, 1), 15: (H, 0), 16: (H, 1)}
ROWSUMS = {2: (0,), 3: (1,), 4: (2, 3)}
ROW_SCALE = 7
WRITE_OUT = {6: (0, 1, 2, 3)}

SLOPE = 0.2
ZERO_ROW = 1e-6
CLAMP_HI = 9e13
NEG_PENALTY = 9e15
BIG = 3e38
EPS = 1e-5
FOLD_STEPS = 6

NEXT_JOBS = {5: "f2", 6: "f1", 7: "sp0", 8: "sp1"}
PREV_JOBS = {4: "heads", 9: "x1t", 10: "q", 11: "k", 12: "v", 16: "o0", 17: "o1", 18: "o2", 19: "o3"}


VECTOR_JOBS = ("heads", "o0", "o1", "o2", "o3")


def side_jobs(has_prev, has_next):
    jobs = {}
    if has_next:
        jobs.update(NEXT_JOBS)
    if has_prev:
        jobs.update(PREV_JOBS)
    return dict(sorted(jobs.items()))


NEXT_ORDER = [job for _, job in sorted({**NEXT_JOBS, **PREV_JOBS}.items())]


class Turn:

    def __init__(self, g, parity):
        self.g, self.p = g, parity
        fixed = isinstance(g, int)
        self.heads = not fixed or 0 <= g < GRAPHS
        self.prev = not fixed or g >= 1
        self.next = not fixed or g < GRAPHS - 1
        self.fixed = fixed
        jobs = side_jobs(self.prev, self.next)
        self.job = jobs
        order = {name: i for i, name in enumerate(jobs.values())}
        full = len(side_jobs(True, True))
        part = len(NEXT_JOBS)
        if fixed and g < 1:
            base = part * (g + 1)
        elif fixed and g == GRAPHS:
            base = 2 * part + full * (GRAPHS - 2) + len(PREV_JOBS)
        else:
            base = g * full + (2 * part - full)
        self.side = {name: base + i for name, i in order.items()}
        self.side_base = base
        self.xT_used = base if fixed and g < 2 else base - (full - 1 - NEXT_ORDER.index("sp1"))

    def has_tile(self, s):
        if s < 0:
            return self.prev
        dense = DENSE <= s < DENSE + NB
        return self.prev if dense else self.heads

    def due_now(self, s, lag):
        found = [r for r in range(-NB, SLOTS)
                 if self.has_tile(r) and r + lag["dense" if DENSE <= r < DENSE + NB else "head"] == s]
        return found

    def tile(self, s):
        if self.fixed and self.g == 0:
            return s if s < DENSE else s - NB
        if self.fixed and self.g == GRAPHS:
            return (SLOTS * GRAPHS - NB) + (s if s <= 0 else s - DENSE)
        return self.g * SLOTS + (s - NB)

    def head_tile(self, s):
        return self.g * (H * NB) + (s if s < DENSE else s - NB)

    def group(self, s):
        return (self.p + s // NB) % 2

    def groups_used(self, s):
        if self.fixed and self.g == GRAPHS and s >= DENSE:
            return GRAPHS * H
        return self.g * H + {0: -2, 1: 0, 2: 1, 3: 2, 4: 3}[s // NB]

    def unit(self, h):
        return self.g * H + h


def turns(eng):
    for g in (-1, 0, 1):
        yield Turn(g, g % 2)
    with eng.Fori(0, (GRAPHS - 4) // 2) as step:
        yield Turn(step * 2 + 2, 0)
        yield Turn(step * 2 + 3, 1)
    for g in (GRAPHS - 2, GRAPHS - 1, GRAPHS):
        yield Turn(g, g % 2)


def due(count):
    return not isinstance(count, int) or count > 0


def build(nc, x, xT, adj, w0, u0, v0, bias0, projT, proj_b, wvT, bv, wkT, bk, wqT, bq, out):
    with ExitStack() as ctx:
        def sb(name, shape, dt=F32):
            return ctx.enter_context(nc.sbuf_tensor(name, shape, dt))

        def ps(name, shape, dt=F32):
            return ctx.enter_context(nc.psum_tensor(name, shape, dt))

        def sem(name):
            return ctx.enter_context(nc.semaphore(name))

        f2_dram = nc.dram_tensor("f2_rows", [2, H, N], F32, kind="Internal").ap()

        ident = sb("ident", [P, P])
        wp = sb("wp", [P, 2 * P])
        uv_row = sb("uv_row", [P, 2, P])
        wuv = sb("wuv", [P, 2, P])
        w_f1 = sb("w_f1", [P, H])
        w_f2 = sb("w_f2", [P, H])
        bias_rows = sb("bias_rows", [P, 2, P])
        bias_row = sb("bias_row", [P, P])
        wv_sb = sb("wv_sb", [P, P])
        wk_sb = sb("wk_sb", [P, P])
        wq_sb = sb("wq_sb", [P, P])
        bv_row = sb("bv_row", [P, P])
        bq_col = sb("bq_col", [P, 1])
        bk_col = sb("bk_col", [P, 1])
        half = sb("half", [P, NB])

        x_sb = [sb(f"x_sb{i}", [P, NB, F]) for i in range(2)]
        xT_sb = sb("xT_sb", [P, N])
        adj_sb = [sb(f"adj_sb{i}", [P, NB, N]) for i in range(2)]
        adj_r = [sb(f"adj_r{i}", [P, NB, N], F32R) for i in range(2)]
        cap = sb("cap", [P, NB, N])
        rowsum = sb("rowsum", [P, NB])
        row_zero = sb("row_zero", [P, NB])
        row_scale = [sb(f"row_scale{i}", [P, NB]) for i in range(2)]
        f1_raw = sb("f1_raw", [P, NB, H])
        f1 = [sb(f"f1_{i}", [P, NB, H]) for i in range(2)]
        f2_row = sb("f2_row", [H, N])
        f2_all = [sb(f"f2_all{i}", [P, H, N]) for i in range(2)]
        xw = [sb(f"xw{i}", [P, NB, 2 * P]) for i in range(2)]
        support = [t[:, :, 0:P] for t in xw]
        skip = [t[:, :, P:2 * P] for t in xw]
        neg_max = [sb(f"neg_max{i}", [P, NB, H]) for i in range(2)]
        sums = [sb(f"sums{i}", [P, NB, H]) for i in range(2)]

        w = [sb(f"w{i}", [P, NB, N]) for i in range(2)]
        w_hi = [sb(f"w_hi{i}", [P, NB, N], F32R) for i in range(2)]
        w_lo = [sb(f"w_lo{i}", [P, NB, N], F32R) for i in range(2)]

        zero_pen = [sb(f"zero_pen{i}", [P, N], BF16) for i in range(2)]
        neg_h = [sb(f"neg_h{i}", [P, N]) for i in range(RING)]
        prob = [sb(f"prob{i}", [P, N]) for i in range(RING)]
        probT = [sb(f"probT{i}", [P, NB, N]) for i in range(2)]
        scrap = sb("scrap", [P, N], BF16)

        headsT_sb = sb("headsT_sb", [P, H, P])
        recip = sb("recip", [P, NB, H])
        head_scale = sb("head_scale", [P, NB, H])
        att = sb("att", [P, NB, P])
        pre = sb("pre", [P, NB, P])
        th = sb("th", [P, NB, P])
        y = sb("y", [P, NB, P])
        stats = sb("stats", [P, NB, 6])
        mean_var = sb("mean_var", [P, NB, 2])
        var_eps = sb("var_eps", [P, NB])
        rstd = sb("rstd", [P, NB])
        x1 = sb("x1", [P, NB, P])
        x1T = sb("x1T", [P, N])
        qT = sb("qT", [P, N])
        kT = sb("kT", [P, N])
        v_pre = sb("v_pre", [P, NB, P])
        v_biased = sb("v_biased", [P, NB, P])
        v_sb = sb("v_sb", [P, NB, P])
        d_max = sb("d_max", [P, NB])
        d_neg_max = sb("d_neg_max", [P, NB])
        d_sums = sb("d_sums", [P, NB])
        d_recip = sb("d_recip", [P, NB])
        y2 = sb("y2", [P, NB, P])
        stats2 = sb("stats2", [P, NB, 6])
        mean_var2 = sb("mean_var2", [P, NB, 2])
        var_eps2 = sb("var_eps2", [P, NB])
        rstd2 = sb("rstd2", [P, NB])
        out_sb = sb("out_sb", [P, NB, P])

        score = [ps(f"score{i}", [P, N]) for i in range(RING)]
        flip = [ps(f"flip{i}", [P, N]) for i in range(2)]
        headsT = ps("headsT", [P, H, P])
        side = ps("side", [P, N])

        s_weights = sem("weights_loaded")
        s_x = [sem(f"x_loaded{i}") for i in range(2)]
        s_xT = sem("xT_loaded")
        s_adj = [sem(f"adj_loaded{i}") for i in range(2)]
        s_f2_stored = sem("f2_stored")
        s_f2_all = [sem(f"f2_all_loaded{i}") for i in range(2)]
        s_stored = sem("out_stored")
        s_ident = sem("ident_ready")
        s_fold = sem("folded_weights_steps")
        s_score = sem("score_done")
        s_flip = sem("flip_done")
        s_value = sem("value_done")
        s_headsT = sem("headsT_copied")
        s_side = sem("side_done")
        s_side_read = sem("side_read")
        s_pen = sem("zero_pen_ready")
        s_masked = sem("masked_ready")
        s_dmax = sem("dense_max_steps")
        s_exp = sem("exp_done")
        s_probT = sem("probT_ready")
        s_logit = sem("logit_ready")
        s_lrelu = sem("lrelu_done")
        s_hi = sem("w_hi_ready")
        s_lo = sem("w_lo_ready")
        s_f1 = sem("f1_ready")
        s_rowsum = sem("rowsum_ready")
        s_rows = sem("row_scale_ready")
        s_adj_r = sem("adj_r_ready")
        s_cap = sem("cap_ready")
        s_recip = sem("recip_steps")
        s_skip = sem("skip_ready")
        s_pre = sem("pre_ready")
        s_tanh = sem("tanh_done")
        s_y = sem("y_ready")
        s_stats = sem("stats_steps")
        s_eps = sem("var_eps_ready")
        s_rstd = sem("rstd_ready")
        s_x1 = sem("x1_ready")
        s_vb = sem("v_biased_ready")
        s_v = sem("v_ready")
        s_dinv = sem("dense_recip_ready")
        s_stats2 = sem("stats2_steps")
        s_y2 = sem("y2_ready")
        s_eps2 = sem("var_eps2_ready")
        s_rstd2 = sem("rstd2_ready")
        s_out = sem("out_ready")

        WEIGHT_LOADS = 12
        weights_loaded = 16 * WEIGHT_LOADS

        def loads(graph, parity):
            return (graph - parity) * 8 + 16

        def rows(dram, graph):
            return dram[bass.ds(graph, 1)].rearrange("o (b p) f -> p (o b) f", p=P)

        block = ctx.enter_context(nc.Block())

        @block.sync
        def _(sp):
            def load(dst, src):
                sp.dma_start(dst, src).then_inc(s_weights, 16)

            load(wp[:, 0:P], w0)
            load(wp[:, P:2 * P], projT)
            load(uv_row[:, 0, :], u0.broadcast_to([P, P]))
            load(uv_row[:, 1, :], v0.broadcast_to([P, P]))
            load(bias_rows[:, 0, :], bias0.broadcast_to([P, P]))
            load(bias_rows[:, 1, :], proj_b.broadcast_to([P, P]))
            load(wv_sb[:], wvT)
            load(wk_sb[:], wkT)
            load(wq_sb[:], wqT)
            load(bv_row[:], bv.broadcast_to([P, P]))
            load(bq_col[:], bq)
            load(bk_col[:], bk)

            for t in turns(sp):
                g, q = t.g, 1 - t.p
                if t.next:
                    if due(t.xT_used):
                        sp.wait_ge(s_side, t.xT_used)
                        sp.nop(nofuse=True)
                    sp.dma_start(xT_sb[:], xT[bass.ds(g + 1, 1)].rearrange("o f n -> (o f) n")).then_inc(s_xT, 16)
                    if t.prev:
                        sp.wait_ge(s_cap, g)
                        sp.nop(nofuse=True)
                    sp.dma_start(adj_sb[q][:], rows(adj, g + 1)).then_inc(s_adj[q], 16)
                    sp.wait_ge(s_side_read, t.side["f2"] + 1)
                    sp.nop(nofuse=True)
                    sp.dma_start(f2_dram[q], f2_row[:]).then_inc(s_f2_stored, 16)
                    sp.wait_ge(s_f2_stored, (g + 2) * 16)
                    sp.nop(nofuse=True)
                    if t.prev:
                        sp.wait_ge(s_logit, g * H * NB)
                        sp.nop(nofuse=True)
                    sp.dma_start(f2_all[q][:], f2_dram[q:q + 1].broadcast_to([P, H, N])).then_inc(s_f2_all[q], 16)
                    if t.prev:
                        sp.wait_ge(s_y, g)
                        sp.nop(nofuse=True)
                    sp.dma_start(x_sb[q][:], rows(x, g + 1)).then_inc(s_x[q], 16)
                if not t.fixed or g >= 2:
                    sp.wait_ge(s_out, g - 1)
                    sp.nop(nofuse=True)
                    sp.dma_start(rows(out, g - 2), out_sb[:]).then_inc(s_stored, 16)
            sp.wait_ge(s_out, GRAPHS)
            sp.dma_start(rows(out, GRAPHS - 1), out_sb[:]).then_inc(s_stored, 16)
            sp.wait_ge(s_stored, 16 * GRAPHS)

        @block.tensor
        def _(pe):
            def head_scores(t, s, h, i):
                n, k = t.tile(s), h % 2
                if i == 0:
                    pe.wait_ge(s_lo, HALVES * (t.unit(h) + 1))
                    if h == 0:
                        pe.wait_ge(s_adj_r, t.g + 1)
                if due(n - RING + 1):
                    pe.wait_ge(s_masked, n - RING + 1)
                for part in (w_hi[k], w_lo[k]):
                    for b in range(NB):
                        mm = nc.tensor.matmul(score[s % RING][:], part[:, b, i * P:(i + 1) * P], adj_r[t.p][:, b, :],
                                              start=(part is w_hi[k] and b == 0),
                                              stop=(part is w_lo[k] and b == NB - 1))
                mm.then_inc(s_score, 1)

            def dense_scores(t, s, i):
                pe.wait_ge(s_side_read, t.side["k"] + 1)
                pe.wait_ge(s_masked, t.tile(s) - RING + 1)
                nc.tensor.matmul(score[s % RING][:], qT[:, i * P:(i + 1) * P], kT[:],
                                 start=True, stop=True).then_inc(s_score, 1)

            def flip_tile(t, s):
                n = t.tile(s)
                pe.wait_ge(s_exp, n + 1)
                if due(n - 1):
                    pe.wait_ge(s_probT, n - 1)
                for b in range(NB):
                    mm = nc.tensor.transpose(flip[s % 2][:, b * P:(b + 1) * P], prob[s % RING][:, b * P:(b + 1) * P],
                                             ident[:])
                mm.then_inc(s_flip, 1)

            def head_values(t, s):
                h, p = (3, 1 - t.p) if s < 0 else (UNITS[s - s % NB], t.p)
                pe.wait_ge(s_probT, t.tile(s) + 1)
                if h == 0 and due(t.g):
                    pe.wait_ge(s_headsT, t.g)
                for b in range(NB):
                    for i in range(NB):
                        mm = nc.tensor.matmul(headsT[i * D:(i + 1) * D, h, :], support[p][:, b, h * D:(h + 1) * D],
                                              probT[t.group(s)][:, i, b * P:(b + 1) * P],
                                              start=(b == 0), stop=(b == NB - 1), tile_position=(0, i * D))
                mm.then_inc(s_value, 1)

            def side_job(t, s):
                name = t.job[s]
                if name in ("f2", "sp0", "sp1", "f1"):
                    pe.wait_ge(s_xT, (t.g + 2) * 16)
                if name == "heads":
                    pe.wait_ge(s_headsT, t.g)
                if name == "x1t":
                    pe.wait_ge(s_x1, t.g)
                if name[0] == "o":
                    pe.wait_ge(s_probT, t.tile(DENSE + int(name[1])) + 1)
                    pe.wait_ge(s_v, t.g)
                if due(t.side[name]):
                    pe.wait_ge(s_side_read, t.side[name])
                if name == "f2":
                    mm = nc.tensor.matmul(side[0:H, :], w_f2[:], xT_sb[:], start=True, stop=True)
                elif name in ("sp0", "sp1"):
                    for b in range(2):
                        at = (2 * int(name[2]) + b) * P
                        mm = nc.tensor.matmul(side[:, b * 2 * P:(b + 1) * 2 * P], xT_sb[:, at:at + P], wp[:],
                                              start=True, stop=True)
                elif name == "f1":
                    for b in range(NB):
                        mm = nc.tensor.matmul(side[:, b * H:(b + 1) * H], xT_sb[:, b * P:(b + 1) * P], w_f1[:],
                                              start=True, stop=True)
                elif name == "heads":
                    for h in range(H):
                        mm = nc.tensor.transpose(side[:, h * P:(h + 1) * P], headsT_sb[:, h, :], ident[:])
                elif name == "x1t":
                    for b in range(NB):
                        mm = nc.tensor.transpose(side[:, b * P:(b + 1) * P], x1[:, b, :], ident[:])
                elif name in ("q", "k"):
                    mm = nc.tensor.matmul(side[:], (wq_sb if name == "q" else wk_sb)[:], x1T[:], start=True, stop=True)
                elif name == "v":
                    for b in range(NB):
                        mm = nc.tensor.matmul(side[:, b * P:(b + 1) * P], x1T[:, b * P:(b + 1) * P], wv_sb[:],
                                              start=True, stop=True)
                else:
                    i = int(name[1])
                    for b in range(NB):
                        mm = nc.tensor.matmul(side[:, 0:P], probT[t.group(DENSE)][:, i, b * P:(b + 1) * P], v_sb[:, b, :],
                                              start=(b == 0), stop=(b == NB - 1))
                mm.then_inc(s_side, 1)

            pe.wait_ge(s_ident, 2)
            pe.wait_ge(s_weights, weights_loaded)
            pe.wait_ge(s_fold, FOLD_STEPS)
            for t in turns(pe):
                for s in range(SLOTS):
                    if t.has_tile(s):
                        if DENSE <= s < DENSE + NB:
                            dense_scores(t, s, s - DENSE)
                        else:
                            head_scores(t, s, UNITS[s - s % NB], s % NB)
                    if s in t.job and t.job[s][0] != "o":
                        side_job(t, s)
                    for r in t.due_now(s, LAG_T):
                        flip_tile(t, r)
                    for r in t.due_now(s, LAG_V):
                        if DENSE <= r < DENSE + NB:
                            side_job(t, s)
                        elif r % NB == NB - 1:
                            head_values(t, r)

        @block.scalar
        def _(act):
            def side_out(t, name):
                act.wait_ge(s_side, t.side[name] + 1)
                if name == "f2":
                    if due((t.g + 1) * 16):
                        act.wait_ge(s_f2_stored, (t.g + 1) * 16)
                    op = nc.scalar.copy(f2_row[:], side[0:H, :])
                elif name == "f1":
                    if due(t.g + 1):
                        act.wait_ge(s_f1, t.g + 1)
                    op = nc.scalar.copy(f1_raw[:], side[:, 0:NB * H].rearrange("p (b h) -> p b h", b=NB))
                elif name == "x1t":
                    op = nc.scalar.copy(x1T[:], side[:])
                elif name == "q":
                    op = nc.scalar.activation(qT[:], side[:], ACT.Relu, bias=bq_col[:, 0:1])
                elif name == "k":
                    op = nc.scalar.activation(kT[:], side[:], ACT.Relu, bias=bk_col[:, 0:1])
                elif name == "v":
                    if due(t.g - 1):
                        act.wait_ge(s_vb, t.g - 1)
                    op = nc.scalar.copy(v_pre[:], side[:].rearrange("p (b n) -> p b n", b=NB))
                else:
                    at = 2 * int(name[2])
                    if t.prev:
                        act.wait_ge(s_pre, t.g)
                    op = nc.scalar.copy(xw[1 - t.p][:, at:at + 2, :], side[:].rearrange("p (b n) -> p b n", b=2))
                op.then_inc(s_side_read, 1)

            def exp_tile(t, s):
                n = t.tile(s)
                act.wait_ge(s_masked, n + 1)
                if due(n - RING + 1):
                    act.wait_ge(s_flip, n - RING + 1)
                if DENSE <= s < DENSE + NB:
                    i = s - DENSE
                    op = nc.scalar.activation(prob[s % RING][:], neg_h[s % RING][:], ACT.Exp,
                                              bias=d_neg_max[:, i:i + 1], accum_out=d_sums[:, i:i + 1])
                else:
                    h, i = UNITS[s - s % NB], s % NB
                    op = nc.scalar.activation(prob[s % RING][:], neg_h[s % RING][:], ACT.Exp, scale=-1.0,
                                              bias=neg_max[t.p][:, i, h:h + 1], accum_out=sums[t.p][:, i, h:h + 1])
                op.then_inc(s_exp, 1)

            def copy_flipped(t, s):
                act.wait_ge(s_flip, t.tile(s) + 1)
                if s % NB == 0:
                    if 0 <= s < NB and due(t.side_base):
                        act.wait_ge(s_side, t.side_base)
                    if due(t.groups_used(s)):
                        act.wait_ge(s_value, t.groups_used(s))
                nc.scalar.copy(probT[t.group(s)][:, s % NB, :], flip[s % 2][:]).then_inc(s_probT, 1)

            def logits(t, graph, p, h, b):
                u = graph * H + h
                if b == 0:
                    if due(u - 1):
                        act.wait_ge(s_lo, HALVES * (u - 1))
                    if h == 0:
                        act.wait_ge(s_f2_all[p], loads(graph, p))
                        act.wait_ge(s_f1, graph + 1)
                nc.scalar.activation(w[h % 2][:, b, :], f2_all[p][:, h, :], ACT.Identity,
                                     scale=row_scale[p][:, b:b + 1], bias=f1[p][:, b, h:h + 1]).then_inc(s_logit, 1)

            act.wait_ge(s_weights, weights_loaded)
            for t in turns(act):
                g, q = t.g, 1 - t.p
                for s in range(SLOTS):
                    if s in t.job and t.job[s] not in VECTOR_JOBS:
                        side_out(t, t.job[s])
                    for unit, b in LOGITS.get(s, ()):
                        if unit < H and t.heads:
                            logits(t, g, t.p, unit, b)
                        elif unit >= H and t.next:
                            logits(t, g + 1, q, unit - H, b)
                    if s == 3 and t.prev:
                        act.wait_ge(s_value, g * H)
                        if due(t.side_base):
                            act.wait_ge(s_side, t.side_base)
                        nc.scalar.copy(headsT_sb[:], headsT[:]).then_inc(s_headsT, 1)
                    if t.has_tile(s):
                        exp_tile(t, s)
                    for r in t.due_now(s, LAG_C):
                        copy_flipped(t, r)
                    if s in ROWSUMS and t.next:
                        for b in ROWSUMS[s]:
                            if b == 0:
                                act.wait_ge(s_adj[q], loads(g + 1, q))
                                if due(2 * (g + 1)):
                                    act.wait_ge(s_rows, 2 * (g + 1))
                            if due(NB * (g + 1) + b):
                                act.wait_ge(s_rowsum, NB * (g + 1) + b)
                            nc.scalar.activation(scrap[:], adj_sb[q][:, b, :], ACT.Identity,
                                                 accum_out=rowsum[:, b:b + 1]).then_inc(s_rowsum, 1)
                    if s == 5 and t.prev:
                        act.wait_ge(s_pre, g)
                        nc.scalar.activation(th[:], pre[:], ACT.Tanh).then_inc(s_tanh, 1)

        @block.vector
        def _(dve):
            def find_zeros(t, s):
                n = t.tile(s)
                dve.wait_ge(s_score, n + 1)
                if due(n - 1):
                    dve.wait_ge(s_masked, n - 1)
                nc.vector.tensor_scalar(zero_pen[s % 2][:], score[s % RING][:], 0.0, -BIG, ALU.is_equal,
                                        ALU.mult).then_inc(s_pen, 1)

            def mask_head(t, s):
                n, m, h, i = t.tile(s), t.head_tile(s), UNITS[s - s % NB], s % NB
                if due(n - RING + 1):
                    dve.wait_ge(s_exp, n - RING + 1)
                dve.wait_ge(s_pen, m + 1)
                dve.nop(nofuse=True)
                nc.vector.tensor_tensor_reduce(neg_h[s % RING][:], score[s % RING][:], zero_pen[s % 2][:], -1.0, BIG,
                                               ALU.add, ALU.min, neg_max[t.p][:, i, h:h + 1]).then_inc(s_masked, 1)

            def mask_dense(t, s):
                n, i = t.tile(s), s - DENSE
                step = 2 * (NB * (t.g - 1) + i)
                dve.wait_ge(s_score, n + 1)
                dve.wait_ge(s_exp, n - RING + 1)
                if i == 0:
                    dve.wait_ge(s_cap, t.g)
                nc.vector.scalar_tensor_tensor(out=neg_h[s % RING][:], in0=score[s % RING][:], scalar=CLAMP_HI,
                                               in1=cap[:, i, :], op0=ALU.min, op1=ALU.min).then_inc(s_dmax, 1)
                dve.wait_ge(s_dmax, step + 1)
                nc.vector.tensor_reduce(d_max[:, i:i + 1], neg_h[s % RING][:], AX_X, ALU.max).then_inc(s_dmax, 1)
                dve.wait_ge(s_dmax, step + 2)
                nc.vector.tensor_scalar(d_neg_max[:, i:i + 1], d_max[:, i:i + 1], -1.0, None,
                                        ALU.mult).then_inc(s_masked, 1)

            def leaky_relu(unit, h, b):
                mine = w[h % 2][:, b, :]
                dve.wait_ge(s_logit, NB * unit + b + 1)
                nc.vector.scalar_tensor_tensor(out=mine, in0=mine, scalar=SLOPE, in1=mine, op0=ALU.mult, op1=ALU.max)\
                    .then_inc(s_lrelu, 1)

            def round_half(unit, h, half_no, free):
                lo, hi = half_no * (NB // HALVES), (half_no + 1) * (NB // HALVES)
                if half_no == 0 and due(free):
                    dve.wait_ge(s_score, free)
                dve.wait_ge(s_lrelu, NB * unit + hi)
                nc.vector.tensor_copy(w_hi[h % 2][:, lo:hi, :], w[h % 2][:, lo:hi, :]).then_inc(s_hi, 1)

            def leaky_at(t, s):
                for unit, b in LEAKY.get(s, ()):
                    if t.next if unit >= H else t.heads:
                        leaky_relu(t.unit(unit), unit % H, b)

            def round_at(t, s):
                unit, half_no = ROUND[s]
                if t.next if unit >= H else t.heads:
                    before = {1: -1, 2: 3, 3: 7, H: 11}[unit]
                    round_half(t.unit(unit), unit % H, half_no, t.tile(before) + 1 if t.heads else 0)

            def head_scales(t):
                g, o = t.g, 1 - t.p
                dve.wait_ge(s_exp, t.tile(0))
                if due(g - 1):
                    dve.wait_ge(s_side_read, t.side_base)
                nc.vector.reciprocal(recip[:], sums[o][:]).then_inc(s_recip, 1)
                dve.wait_ge(s_recip, 2 * g - 1)
                nc.vector.scalar_tensor_tensor(out=head_scale[:], in0=neg_max[o][:], scalar=0.5 * BIG, in1=recip[:],
                                               op0=ALU.is_lt, op1=ALU.mult).then_inc(s_recip, 1)

            def row_stats(src, into, total, s_steps, g):
                for b in range(NB):
                    op = nc.vector.bn_stats(into[:, b, :], src[:, b, :])
                op.then_inc(s_steps, 1)
                dve.wait_ge(s_steps, 2 * g - 1)
                dve.nop(nofuse=True)
                for b in range(NB):
                    op = nc.vector.bn_aggr(total[:, b, :], into[:, b, :])
                op.then_inc(s_steps, 1)

            def write_out(graph, blocks):
                if blocks[0] == 0:
                    dve.wait_ge(s_rstd2, graph + 1)
                    if due(graph):
                        dve.wait_ge(s_stored, 16 * graph)
                for b in blocks:
                    op = nc.vector.tensor_scalar(out_sb[:, b, :], y2[:, b, :], mean_var2[:, b, 0:1],
                                                 rstd2[:, b:b + 1], ALU.subtract, ALU.mult)
                if b == NB - 1:
                    op.then_inc(s_out, 1)

            def centre_x1():
                for b in range(NB):
                    op = nc.vector.tensor_scalar(x1[:, b, :], y[:, b, :], mean_var[:, b, 0:1], rstd[:, b:b + 1],
                                                 ALU.subtract, ALU.mult)
                op.then_inc(s_x1, 1)

            def side_out(t, name):
                dve.wait_ge(s_side, t.side[name] + 1)
                if name == "heads":
                    dve.wait_ge(s_recip, 2 * t.g)
                    if due(t.g - 1):
                        dve.wait_ge(s_pre, t.g - 1)
                    nc.vector.tensor_tensor(att[:].rearrange("p b (h d) -> p b h d", h=H),
                                            side[:].rearrange("p (h b d) -> p b h d", h=H, b=NB),
                                            head_scale[:].rearrange("p b (h o) -> p b h o", o=1)
                                            .broadcast_to([P, NB, H, D]), ALU.mult).then_inc(s_side_read, 1)
                else:
                    i = int(name[1])
                    if i == 0:
                        if due(t.g - 1):
                            dve.wait_ge(s_out, t.g - 1)
                    nc.vector.reciprocal(d_recip[:, i:i + 1], d_sums[:, i:i + 1]).then_inc(s_dinv, 1)
                    dve.wait_ge(s_dinv, NB * (t.g - 1) + i + 1)
                    nc.vector.scalar_tensor_tensor(out=y2[:, i, :], in0=side[:, 0:P], scalar=d_recip[:, i:i + 1],
                                                   in1=x1[:, i, :], op0=ALU.mult, op1=ALU.add)\
                        .then_inc(s_side_read, 1)

            dve.wait_ge(s_weights, weights_loaded)
            nc.vector.memset(half[:], -0.5).then_inc(s_fold, 1)
            nc.vector.tensor_tensor(bias_row[:], bias_rows[:, 0, :], bias_rows[:, 1, :], ALU.add).then_inc(s_fold, 1)
            for k in range(2):
                nc.vector.tensor_tensor(wuv[:, k, :], wp[:, 0:P], uv_row[:, k, :], ALU.mult).then_inc(s_fold, 1)
            dve.wait_ge(s_fold, 4)
            for k, folded in enumerate((w_f1, w_f2)):
                nc.vector.tensor_reduce(folded[:], wuv[:, k, :].rearrange("p (h d) -> p h d", h=H), AX_X,
                                        ALU.add).then_inc(s_fold, 1)

            for t in turns(dve):
                g, q = t.g, 1 - t.p
                for s in range(SLOTS):
                    if s == 7 and t.prev:
                        dve.wait_ge(s_y, g)
                        if due(g - 1):
                            dve.wait_ge(s_x1, g - 1)
                        row_stats(y, stats, mean_var, s_stats, g)
                    if s == ROW_SCALE and t.next:
                        dve.wait_ge(s_rowsum, NB * (g + 2))
                        if due(g + 1):
                            dve.wait_ge(s_adj_r, g + 1)
                        nc.vector.tensor_scalar(row_zero[:], rowsum[:], 0.0, None, ALU.is_equal).then_inc(s_rows, 1)
                        if t.prev:
                            dve.wait_ge(s_logit, g * H * NB)
                        nc.vector.tensor_scalar(row_scale[q][:], rowsum[:], 0.0, ZERO_ROW, ALU.is_gt,
                                                ALU.max).then_inc(s_rows, 1)
                        dve.wait_ge(s_side_read, t.side["f1"] + 1)
                        dve.wait_ge(s_rows, 2 * (g + 2))
                        nc.vector.tensor_tensor(f1[q][:], f1_raw[:], row_scale[q][:].rearrange("p (b o) -> p b o", o=1)
                                                .broadcast_to([P, NB, H]), ALU.mult).then_inc(s_f1, 1)
                    if s == 0:
                        round_at(t, s)
                    dense = DENSE <= s < DENSE + NB
                    if t.has_tile(s) and not dense:
                        find_zeros(t, s)
                    leaky_at(t, s)
                    if t.has_tile(s):
                        (mask_dense if dense else mask_head)(t, s)
                    if t.job.get(s) in VECTOR_JOBS:
                        side_out(t, t.job[s])
                    if s > 0 and s in ROUND:
                        round_at(t, s)
                    if s == 8 and t.prev:
                        dve.wait_ge(s_rstd, g)
                        dve.wait_ge(s_side_read, t.side_base)
                        centre_x1()
                    if s in WRITE_OUT and (not t.fixed or g >= 2):
                        write_out(g - 2, WRITE_OUT[s])
                    if s == 3 and t.prev:
                        head_scales(t)
                    if s == 19 and t.prev:
                        dve.wait_ge(s_side_read, t.side["o3"] + 1)
                        row_stats(y2, stats2, mean_var2, s_stats2, g)
            write_out(GRAPHS - 1, range(NB))

        @block.gpsimd
        def _(pool):
            def split_lo(unit, h, half_no):
                part = slice(half_no * (NB // HALVES), (half_no + 1) * (NB // HALVES))
                pool.wait_ge(s_hi, HALVES * unit + half_no + 1)
                nc.gpsimd.tensor_tensor(w_lo[h % 2][:, part, :], w[h % 2][:, part, :],
                                        w_hi[h % 2][:, part, :].bitcast(F32), ALU.subtract).then_inc(s_lo, 1)

            def inverse_std(total, shifted, scale, s_steps, s_shift, done, g):
                pool.wait_ge(s_steps, 2 * g)
                pool.nop(nofuse=True)
                nc.gpsimd.tensor_scalar(shifted[:], total[:, :, 1], EPS, None, ALU.add).then_inc(s_shift, 1)
                pool.wait_ge(s_shift, g)
                nc.gpsimd.tensor_tensor(scale[:], shifted[:], half[:], ALU.pow).then_inc(done, 1)

            nc.gpsimd.memset(ident[:], 0.0).then_inc(s_ident, 1)
            pool.wait_ge(s_ident, 1)
            nc.gpsimd.affine_select(out=ident[:], in_=ident[:], compare_op=ALU.not_equal, fill=1.0, base=0,
                                    pattern=[[-1, P]], channel_multiplier=1).then_inc(s_ident, 1)
            pool.wait_ge(s_fold, FOLD_STEPS)

            for t in turns(pool):
                g, q = t.g, 1 - t.p
                if t.heads:
                    split_lo(t.unit(1), 1, 0)
                    split_lo(t.unit(1), 1, 1)
                if t.prev:
                    pool.wait_ge(s_skip, g)
                    pool.wait_ge(s_side_read, t.side["heads"] + 1)
                    if due(g - 1):
                        pool.wait_ge(s_tanh, g - 1)
                    nc.gpsimd.tensor_tensor(pre[:], att[:], skip[q], ALU.add).then_inc(s_pre, 1)
                if t.heads:
                    split_lo(t.unit(2), 2, 0)
                    split_lo(t.unit(2), 2, 1)
                if t.prev:
                    pool.wait_ge(s_tanh, g)
                    pool.wait_ge(s_x[q], loads(g - 1, q))
                    if due(g - 1):
                        pool.wait_ge(s_x1, g - 1)
                    nc.gpsimd.tensor_tensor(y[:], x_sb[q][:], th[:], ALU.add).then_inc(s_y, 1)
                    inverse_std(mean_var, var_eps, rstd, s_stats, s_eps, s_rstd, g)
                if t.next:
                    pool.wait_ge(s_side_read, t.side["sp1"] + 1)
                    nc.gpsimd.tensor_tensor(skip[q], skip[q],
                                            bias_row[:].rearrange("p (o n) -> p o n", o=1).broadcast_to([P, NB, P]),
                                            ALU.add).then_inc(s_skip, 1)
                if t.next:
                    pool.wait_ge(s_rows, 2 * (g + 2))
                    if t.prev:
                        pool.wait_ge(s_score, t.tile(0))
                    pool.nop(nofuse=True)
                    for b in range(NB):
                        op = nc.gpsimd.tensor_scalar(adj_r[q][:, b, :], adj_sb[q][:, b, :], 1.0,
                                                     row_zero[:, b:b + 1], ALU.mult, ALU.add)
                    op.then_inc(s_adj_r, 1)
                if t.heads:
                    split_lo(t.unit(3), 3, 0)
                    split_lo(t.unit(3), 3, 1)
                if t.prev:
                    pool.wait_ge(s_side_read, t.side["v"] + 1)
                    nc.gpsimd.tensor_tensor(v_biased[:], v_pre[:],
                                            bv_row[:].rearrange("p (o n) -> p o n", o=1).broadcast_to([P, NB, P]),
                                            ALU.add).then_inc(s_vb, 1)
                    pool.wait_ge(s_vb, g)
                    pool.wait_ge(s_side, t.side_base)
                    pool.nop(nofuse=True)
                    nc.gpsimd.tensor_scalar(v_sb[:], v_biased[:], 0.0, None, ALU.max).then_inc(s_v, 1)
                if t.next:
                    split_lo(t.unit(H), 0, 0)
                if t.heads:
                    pool.wait_ge(s_adj[t.p], loads(g, t.p))
                    if t.prev:
                        pool.wait_ge(s_masked, t.tile(DENSE + NB - 1) + 1)
                    pool.nop(nofuse=True)
                    nc.gpsimd.tensor_scalar(cap[:], adj_sb[t.p][:], 2 * NEG_PENALTY, -NEG_PENALTY, ALU.mult,
                                            ALU.add).then_inc(s_cap, 1)
                if t.next:
                    split_lo(t.unit(H), 0, 1)
                if t.prev:
                    inverse_std(mean_var2, var_eps2, rstd2, s_stats2, s_eps2, s_rstd2, g)


def kernel(x, adj, L0_gnn_weight, L0_gnn_weight_u, L0_gnn_weight_v, L0_gnn_bias, L0_gnn_proj_w, L0_gnn_proj_b,
           L1_gnn_Wv, L1_gnn_bv, L1_gnn_Wk, L1_gnn_bk, L1_gnn_Wq, L1_gnn_bq):
    import numpy as np
    import concourse.bacc as bacc
    from concourse.bass_utils import run_bass_kernel_spmd

    def as_laid(a):
        return np.ascontiguousarray(np.asarray(a))

    arrays = {
        "x": as_laid(x),
        "xT": as_laid(np.asarray(x).transpose(0, 2, 1)),
        "adj": as_laid(adj),
        "w0": as_laid(L0_gnn_weight),
        "u0": as_laid(np.asarray(L0_gnn_weight_u).reshape(1, P)),
        "v0": as_laid(np.asarray(L0_gnn_weight_v).reshape(1, P)),
        "bias0": as_laid(np.asarray(L0_gnn_bias).reshape(1, P)),
        "projT": as_laid(np.asarray(L0_gnn_proj_w).T),
        "proj_b": as_laid(np.asarray(L0_gnn_proj_b).reshape(1, P)),
        "wvT": as_laid(np.asarray(L1_gnn_Wv).T),
        "bv": as_laid(np.asarray(L1_gnn_bv).reshape(1, P)),
        "wkT": as_laid(np.asarray(L1_gnn_Wk).T),
        "bk": as_laid(np.asarray(L1_gnn_bk).reshape(P, 1)),
        "wqT": as_laid(np.asarray(L1_gnn_Wq).T),
        "bq": as_laid(np.asarray(L1_gnn_bq).reshape(P, 1)),
    }
    nc = bacc.Bacc("TRN2", target_bir_lowering=False, num_devices=1)
    aps = {k: nc.dram_tensor(f"in_{k}", a.shape, mybir.dt.from_np(a.dtype), kind="ExternalInput").ap()
           for k, a in arrays.items()}
    out = nc.dram_tensor("out", (GRAPHS, N, F), F32, kind="ExternalOutput").ap()
    build(nc, **aps, out=out)
    result = run_bass_kernel_spmd(nc, [{f"in_{k}": a for k, a in arrays.items()}], core_ids=[0])
    return result.results[0]["out"]
```

```python
from contextlib import ExitStack

import concourse.bass as bass
from concourse import mybir

F32 = mybir.dt.float32
F32R = mybir.dt.float32r
BF16 = mybir.dt.bfloat16
ALU = mybir.AluOpType
ACT = mybir.ActivationFunctionType
AX_X = mybir.AxisListType.X

GRAPHS, N, F = 16, 512, 128
H, D = 4, 32
P = 128
NB = N // P
SLOTS = 20
LAG_T = 3
LAG_C = LAG_T - 1
VALUES = {3: -1, 7: 3, 11: 7, 16: 11}
UNITS = {0: 0, 4: 1, 8: 2, 16: 3}
DENSE = 12
RING = 4

HALVES = 2

LOGITS = {0: ((2, 0), (2, 1)), 1: ((2, 2), (2, 3)), 6: ((3, 0), (3, 1)), 7: ((3, 2),), 8: ((3, 3),),
          9: ((H, 0),), 10: ((H, 1),), 11: ((H, 2),), 13: ((H, 3),),
          15: ((H + 1, 0),), 16: ((H + 1, 1),), 17: ((H + 1, 2),), 18: ((H + 1, 3),)}
LEAKY = {2: ((2, 0),), 3: ((2, 1),), 4: ((2, 2),), 5: ((2, 3),), 9: ((3, 0), (3, 1)),
         10: ((3, 2), (3, 3)), 11: ((H, 0),), 12: ((H, 1),), 13: ((H, 2),), 16: ((H, 3),),
         17: ((H + 1, 0),), 18: ((H + 1, 1), (H + 1, 2)), 19: ((H + 1, 3),)}
ROUND = {0: (1, 0), 1: (1, 1), 4: (2, 0), 5: (2, 1), 10: (3, 0), 11: (3, 1), 16: (H, 0), 17: (H, 1)}
EARLY_LEAKY = {13: ((H, 2), (H, 3)), 16: ()}
EARLY_ROUND = {12: (H, 0), 13: (H, 1)}
ROWSUMS = {2: (0,), 3: (1,), 4: (2,), 5: (3,)}
ROW_SCALE = 7
STATS2 = {17: ("o0", (0,)), 18: ("o1", (1,)), 19: ("o3", (2, 3))}
WRITE_OUT = 8

SLOPE = 0.2
ZERO_ROW = 1e-6
CLAMP_HI = 9e13
NEG_PENALTY = 9e15
BIG = 3e38
EPS = 1e-5
FOLD_STEPS = 6

NEXT_JOBS = {3: "f2", 5: "f1", 7: "sp0", 8: "sp1"}
PREV_JOBS = {4: "heads", 9: "x1t", 10: "q", 11: "k", 12: "v", 16: "o0", 17: "o1", 18: "o2", 19: "o3"}


VECTOR_JOBS = ("heads", "o0", "o1", "o2", "o3")


def side_jobs(has_prev, has_next):
    jobs = {}
    if has_next:
        jobs.update(NEXT_JOBS)
    if has_prev:
        jobs.update(PREV_JOBS)
    return dict(sorted(jobs.items()))


NEXT_ORDER = [job for _, job in sorted({**NEXT_JOBS, **PREV_JOBS}.items())]


class Turn:

    def __init__(self, g, parity):
        self.g, self.p = g, parity
        fixed = isinstance(g, int)
        self.heads = not fixed or 0 <= g < GRAPHS
        self.prev = not fixed or g >= 1
        self.next = not fixed or g < GRAPHS - 1
        self.fixed = fixed
        jobs = side_jobs(self.prev, self.next)
        if fixed and g < 0:
            jobs = {0: "f2", 1: "f1", 17: "sp0", 19: "sp1"}
        self.job = jobs
        self.leaky, self.round = dict(LEAKY), dict(ROUND)
        if fixed and g < 1:
            self.leaky.update(EARLY_LEAKY)
            self.round = {s: which for s, which in ROUND.items() if which[0] < H} | EARLY_ROUND
        order = {name: i for i, name in enumerate(jobs.values())}
        full = len(side_jobs(True, True))
        part = len(NEXT_JOBS)
        if fixed and g < 1:
            base = part * (g + 1)
        elif fixed and g == GRAPHS:
            base = 2 * part + full * (GRAPHS - 2) + len(PREV_JOBS)
        else:
            base = g * full + (2 * part - full)
        self.side = {name: base + i for name, i in order.items()}
        self.side_base = base
        self.xT_used = base if fixed and g < 2 else base - (full - 1 - NEXT_ORDER.index("sp1"))

    def has_tile(self, s):
        if s < 0:
            return self.prev
        dense = DENSE <= s < DENSE + NB
        return self.prev if dense else self.heads

    def due_now(self, s, lag):
        return [s - lag] if self.has_tile(s - lag) else []

    def tile(self, s):
        if self.fixed and self.g == 0:
            return s if s < DENSE else s - NB
        if self.fixed and self.g == GRAPHS:
            return (SLOTS * GRAPHS - NB) + (s if s <= 0 else s - DENSE)
        return self.g * SLOTS + (s - NB)

    def head_tile(self, s):
        return self.g * (H * NB) + (s if s < DENSE else s - NB)

    def group(self, s):
        return (self.p + s // NB) % 2

    def groups_used(self, s):
        if self.fixed and self.g == GRAPHS and s >= DENSE:
            return GRAPHS * H
        return self.g * H + {0: -2, 1: 0, 2: 1, 3: 2, 4: 3}[s // NB]

    def unit(self, h):
        return self.g * H + h


def turns(eng):
    for g in (-1, 0, 1):
        yield Turn(g, g % 2)
    with eng.Fori(0, (GRAPHS - 4) // 2) as step:
        yield Turn(step * 2 + 2, 0)
        yield Turn(step * 2 + 3, 1)
    for g in (GRAPHS - 2, GRAPHS - 1, GRAPHS):
        yield Turn(g, g % 2)


def due(count):
    return not isinstance(count, int) or count > 0


def build(nc, x, xT, adj, w0, u0, v0, bias0, projT, proj_b, wvT, bv, wkT, bk, wqT, bq, out):
    with ExitStack() as ctx:
        def sb(name, shape, dt=F32):
            return ctx.enter_context(nc.sbuf_tensor(name, shape, dt))

        def ps(name, shape, dt=F32):
            return ctx.enter_context(nc.psum_tensor(name, shape, dt))

        def sem(name):
            return ctx.enter_context(nc.semaphore(name))

        f_dram = nc.dram_tensor("f_rows_dram", [2, NB, D, P], F32, kind="Internal").ap()

        ident = sb("ident", [P, P])
        wp = sb("wp", [P, 2 * P])
        uv_row = sb("uv_row", [P, 2, P])
        wuv = sb("wuv", [P, 2, P])
        w_f = sb("w_f", [P, D])
        bias_rows = sb("bias_rows", [P, 2, P])
        bias_row = sb("bias_row", [P, P])
        wv_sb = sb("wv_sb", [P, P])
        wk_sb = sb("wk_sb", [P, P])
        wq_sb = sb("wq_sb", [P, P])
        bv_row = sb("bv_row", [P, P])
        bq_col = sb("bq_col", [P, 1])
        bk_col = sb("bk_col", [P, 1])
        half = sb("half", [P, NB])

        x_sb = [sb(f"x_sb{i}", [P, NB, F]) for i in range(2)]
        xT_sb = sb("xT_sb", [P, N])
        adj_sb = [sb(f"adj_sb{i}", [P, NB, N]) for i in range(2)]
        adj_r = [sb(f"adj_r{i}", [P, NB, N], F32R) for i in range(2)]
        cap = sb("cap", [P, NB, N])
        rowsum = sb("rowsum", [P, NB])
        row_zero = sb("row_zero", [P, NB])
        row_scale = [sb(f"row_scale{i}", [P, NB]) for i in range(2)]
        f1_raw = sb("f1_raw", [P, NB, H])
        f1 = [sb(f"f1_{i}", [P, NB, H]) for i in range(2)]
        f_rows = sb("f_rows", [P, P])
        f2_all = [sb(f"f2_all{i}", [P, H, N]) for i in range(2)]
        xw = [sb(f"xw{i}", [P, NB, 2 * P]) for i in range(2)]
        support = [t[:, :, 0:P] for t in xw]
        skip = [t[:, :, P:2 * P] for t in xw]
        neg_max = [sb(f"neg_max{i}", [P, NB, H]) for i in range(2)]
        sums = [sb(f"sums{i}", [P, NB, H]) for i in range(2)]

        w = [sb(f"w{i}", [P, NB, N]) for i in range(2)]
        w_hi = [sb(f"w_hi{i}", [P, NB, N], F32R) for i in range(2)]
        w_lo = [sb(f"w_lo{i}", [P, NB, N], F32R) for i in range(2)]

        zero_pen = [sb(f"zero_pen{i}", [P, N], BF16) for i in range(2)]
        neg_h = [sb(f"neg_h{i}", [P, N]) for i in range(RING)]
        prob = [sb(f"prob{i}", [P, N]) for i in range(RING)]
        probT = [sb(f"probT{i}", [P, NB, N]) for i in range(2)]
        scrap = sb("scrap", [P, N], BF16)

        headsT_sb = sb("headsT_sb", [P, H, P])
        recip = sb("recip", [P, NB, H])
        head_scale = sb("head_scale", [P, NB, H])
        att = sb("att", [P, NB, P])
        pre = sb("pre", [P, NB, P])
        th = sb("th", [P, NB, P])
        y = sb("y", [P, NB, P])
        stats = sb("stats", [P, NB, 6])
        mean_var = sb("mean_var", [P, NB, 2])
        var_eps = sb("var_eps", [P, NB])
        rstd = sb("rstd", [P, NB])
        x1 = sb("x1", [P, NB, P])
        x1T = sb("x1T", [P, N])
        qT = sb("qT", [P, N])
        kT = sb("kT", [P, N])
        v_pre = sb("v_pre", [P, NB, P])
        v_biased = sb("v_biased", [P, NB, P])
        v_sb = sb("v_sb", [P, NB, P])
        d_max = sb("d_max", [P, NB])
        d_neg_max = sb("d_neg_max", [P, NB])
        d_sums = sb("d_sums", [P, NB])
        d_recip = sb("d_recip", [P, NB])
        y2 = sb("y2", [P, NB, P])
        stats2 = sb("stats2", [P, NB, 6])
        mean_var2 = sb("mean_var2", [P, NB, 2])
        var_eps2 = sb("var_eps2", [P, NB])
        rstd2 = sb("rstd2", [P, NB])
        out_sb = sb("out_sb", [P, NB, P])

        score = [ps(f"score{i}", [P, N]) for i in range(RING)]
        flip = [ps(f"flip{i}", [P, N]) for i in range(2)]
        headsT = ps("headsT", [P, H, P])
        side = ps("side", [P, N])

        s_uv = sem("w0_u_v_loaded")
        s_weights = sem("weights_loaded")
        s_x = [sem(f"x_loaded{i}") for i in range(2)]
        s_xT = sem("xT_loaded")
        s_adj = [sem(f"adj_loaded{i}") for i in range(2)]
        s_f2_stored = sem("f2_stored")
        s_f2_all = [sem(f"f2_all_loaded{i}") for i in range(2)]
        s_stored = sem("out_stored")
        s_ident = sem("ident_ready")
        s_fold = sem("folded_weights_steps")
        s_score = sem("score_done")
        s_flip = sem("flip_done")
        s_value = sem("value_done")
        s_headsT = sem("headsT_copied")
        s_side = sem("side_done")
        s_side_read = sem("side_read")
        s_pen = sem("zero_pen_ready")
        s_masked = sem("masked_ready")
        s_dmax = sem("dense_max_steps")
        s_exp = sem("exp_done")
        s_probT = sem("probT_ready")
        s_logit = sem("logit_ready")
        s_lrelu = sem("lrelu_done")
        s_hi = sem("w_hi_ready")
        s_lo = sem("w_lo_ready")
        s_f1 = sem("f1_ready")
        s_bias = sem("bias_row_ready")
        s_rowsum = sem("rowsum_ready")
        s_rows = sem("row_scale_ready")
        s_adj_r = sem("adj_r_ready")
        s_cap = sem("cap_ready")
        s_recip = sem("recip_steps")
        s_skip = sem("skip_ready")
        s_pre = sem("pre_ready")
        s_tanh = sem("tanh_done")
        s_y = sem("y_ready")
        s_stats = sem("stats_steps")
        s_eps = sem("var_eps_ready")
        s_rstd = sem("rstd_ready")
        s_x1 = sem("x1_ready")
        s_vb = sem("v_biased_ready")
        s_v = sem("v_ready")
        s_dinv = sem("dense_recip_ready")
        s_stats2 = sem("stats2_steps")
        s_eps2 = sem("var_eps2_ready")
        s_rstd2 = sem("rstd2_ready")
        s_out = sem("out_ready")

        WEIGHT_LOADS = 9
        weights_loaded = 16 * WEIGHT_LOADS

        def loads(graph, parity):
            return (graph - parity) * 8 + 16

        def rows(dram, graph):
            return dram[bass.ds(graph, 1)].rearrange("o (b p) f -> p (o b) f", p=P)

        block = ctx.enter_context(nc.Block())

        @block.sync
        def _(sp):
            def load(dst, src):
                sp.dma_start(dst, src).then_inc(s_weights, 16)

            sp.dma_start(wp[:, 0:P], w0).then_inc(s_uv, 16)
            sp.dma_start(uv_row[:, 1, :], v0.broadcast_to([P, P])).then_inc(s_uv, 16)
            sp.dma_start(uv_row[:, 0, :], u0.broadcast_to([P, P])).then_inc(s_uv, 16)

            for t in turns(sp):
                g, q = t.g, 1 - t.p
                if t.next:
                    if due(t.xT_used):
                        sp.wait_ge(s_side, t.xT_used)
                        sp.nop(nofuse=True)
                    sp.dma_start(xT_sb[:], xT[bass.ds(g + 1, 1)].rearrange("o f n -> (o f) n")).then_inc(s_xT, 16)
                    if t.prev:
                        sp.wait_ge(s_cap, g)
                        sp.nop(nofuse=True)
                    sp.dma_start(adj_sb[q][:], rows(adj, g + 1)).then_inc(s_adj[q], 16)
                    sp.wait_ge(s_side_read, t.side["f2"] + 1)
                    sp.nop(nofuse=True)
                    sp.dma_start(f_dram[q].rearrange("b e c -> (b e) c"), f_rows[:]).then_inc(s_f2_stored, 16)
                    sp.wait_ge(s_f2_stored, (g + 2) * 16)
                    sp.nop(nofuse=True)
                    if t.prev:
                        sp.wait_ge(s_logit, g * H * NB)
                        sp.nop(nofuse=True)
                    for h in range(H):
                        sp.dma_start(f2_all[q][:, h, :].rearrange("p (b c) -> p b c", b=NB),
                                     f_dram[q:q + 1, :, h, :].broadcast_to([P, NB, P])).then_inc(s_f2_all[q], 16)
                    if t.fixed and g < 0:
                        load(wp[:, P:2 * P], projT)
                        load(bias_rows[:, 0, :], bias0.broadcast_to([P, P]))
                        load(bias_rows[:, 1, :], proj_b.broadcast_to([P, P]))
                        load(wv_sb[:], wvT)
                        load(wk_sb[:], wkT)
                        load(wq_sb[:], wqT)
                        load(bv_row[:], bv.broadcast_to([P, P]))
                        load(bq_col[:], bq)
                        load(bk_col[:], bk)
                    if t.prev:
                        sp.wait_ge(s_y, g)
                        sp.nop(nofuse=True)
                    sp.dma_start(x_sb[q][:], rows(x, g + 1)).then_inc(s_x[q], 16)
                if not t.fixed or g >= 2:
                    sp.wait_ge(s_out, g - 1)
                    sp.nop(nofuse=True)
                    sp.dma_start(rows(out, g - 2), out_sb[:]).then_inc(s_stored, 16)
            sp.wait_ge(s_out, GRAPHS)
            sp.dma_start(rows(out, GRAPHS - 1), out_sb[:]).then_inc(s_stored, 16)
            sp.wait_ge(s_stored, 16 * GRAPHS)

        @block.tensor
        def _(pe):
            def head_scores(t, s, h, i):
                n, k = t.tile(s), h % 2
                if i == 0:
                    pe.wait_ge(s_lo, HALVES * (t.unit(h) + 1))
                    if h == 0:
                        pe.wait_ge(s_adj_r, t.g + 1)
                if due(n - RING + 1):
                    pe.wait_ge(s_masked, n - RING + 1)
                for part in (w_hi[k], w_lo[k]):
                    for b in range(NB):
                        mm = nc.tensor.matmul(score[s % RING][:], part[:, b, i * P:(i + 1) * P], adj_r[t.p][:, b, :],
                                              start=(part is w_hi[k] and b == 0),
                                              stop=(part is w_lo[k] and b == NB - 1))
                mm.then_inc(s_score, 1)

            def dense_scores(t, s, i):
                pe.wait_ge(s_side_read, t.side["k"] + 1)
                pe.wait_ge(s_masked, t.tile(s) - RING + 1)
                nc.tensor.matmul(score[s % RING][:], qT[:, i * P:(i + 1) * P], kT[:],
                                 start=True, stop=True).then_inc(s_score, 1)

            def flip_tile(t, s):
                n = t.tile(s)
                pe.wait_ge(s_exp, n + 1)
                if due(n - 1):
                    pe.wait_ge(s_probT, n - 1)
                for b in range(NB):
                    mm = nc.tensor.transpose(flip[s % 2][:, b * P:(b + 1) * P], prob[s % RING][:, b * P:(b + 1) * P],
                                             ident[:])
                mm.then_inc(s_flip, 1)

            def head_values(t, s):
                h, p = (3, 1 - t.p) if s < 0 else (UNITS[s - s % NB], t.p)
                pe.wait_ge(s_probT, t.tile(s) + 1)
                if h == 0 and due(t.g):
                    pe.wait_ge(s_headsT, t.g)
                for b in range(NB):
                    for i in range(NB):
                        mm = nc.tensor.matmul(headsT[i * D:(i + 1) * D, h, :], support[p][:, b, h * D:(h + 1) * D],
                                              probT[t.group(s)][:, i, b * P:(b + 1) * P],
                                              start=(b == 0), stop=(b == NB - 1), tile_position=(0, i * D))
                mm.then_inc(s_value, 1)

            def side_job(t, s):
                name = t.job[s]
                if name in ("f2", "sp0", "sp1"):
                    pe.wait_ge(s_xT, (t.g + 2) * 16)
                if name == "heads":
                    pe.wait_ge(s_headsT, t.g)
                if name == "x1t":
                    pe.wait_ge(s_x1, t.g)
                if name[0] == "o":
                    pe.wait_ge(s_probT, t.tile(DENSE + int(name[1])) + 1)
                    pe.wait_ge(s_v, t.g)
                if name == "sp0" and t.fixed and t.g < 0:
                    pe.wait_ge(s_weights, weights_loaded)
                if due(t.side[name]):
                    pe.wait_ge(s_side_read, t.side[name])
                if name == "f2":
                    for b in range(NB):
                        mm = nc.tensor.matmul(side[b * D:(b + 1) * D, 0:P], w_f[:], xT_sb[:, b * P:(b + 1) * P],
                                              start=True, stop=True, tile_position=(0, b * D))
                elif name in ("sp0", "sp1"):
                    for b in range(2):
                        at = (2 * int(name[2]) + b) * P
                        mm = nc.tensor.matmul(side[:, b * 2 * P:(b + 1) * 2 * P], xT_sb[:, at:at + P], wp[:],
                                              start=True, stop=True)
                elif name == "f1":
                    mm = nc.tensor.transpose(side[:, 0:P], f_rows[:], ident[:])
                elif name == "heads":
                    for h in range(H):
                        mm = nc.tensor.transpose(side[:, h * P:(h + 1) * P], headsT_sb[:, h, :], ident[:])
                elif name == "x1t":
                    for b in range(NB):
                        mm = nc.tensor.transpose(side[:, b * P:(b + 1) * P], x1[:, b, :], ident[:])
                elif name in ("q", "k"):
                    mm = nc.tensor.matmul(side[:], (wq_sb if name == "q" else wk_sb)[:], x1T[:], start=True, stop=True)
                elif name == "v":
                    for b in range(NB):
                        mm = nc.tensor.matmul(side[:, b * P:(b + 1) * P], x1T[:, b * P:(b + 1) * P], wv_sb[:],
                                              start=True, stop=True)
                else:
                    i = int(name[1])
                    for b in range(NB):
                        mm = nc.tensor.matmul(side[:, 0:P], probT[t.group(DENSE)][:, i, b * P:(b + 1) * P], v_sb[:, b, :],
                                              start=(b == 0), stop=(b == NB - 1))
                mm.then_inc(s_side, 1)

            pe.wait_ge(s_ident, 2)
            pe.wait_ge(s_fold, FOLD_STEPS)
            for t in turns(pe):
                for s in range(SLOTS):
                    if s == DENSE:
                        for r in t.due_now(s, LAG_T):
                            flip_tile(t, r)
                    if t.has_tile(s):
                        if DENSE <= s < DENSE + NB:
                            dense_scores(t, s, s - DENSE)
                        else:
                            head_scores(t, s, UNITS[s - s % NB], s % NB)
                    if s in t.job and t.job[s][0] != "o":
                        side_job(t, s)
                    if s != DENSE:
                        for r in t.due_now(s, LAG_T):
                            flip_tile(t, r)
                    if t.job.get(s, "")[0:1] == "o":
                        side_job(t, s)
                    if s in VALUES and t.has_tile(VALUES[s]):
                        head_values(t, VALUES[s])

        @block.scalar
        def _(act):
            def side_out(t, name):
                act.wait_ge(s_side, t.side[name] + 1)
                if name == "sp0" and t.fixed and t.g < 0:
                    act.wait_ge(s_weights, weights_loaded)
                if name == "f2":
                    if due((t.g + 1) * 16):
                        act.wait_ge(s_f2_stored, (t.g + 1) * 16)
                    op = nc.scalar.copy(f_rows[:], side[:, 0:P])
                elif name == "f1":
                    if due(t.g + 1):
                        act.wait_ge(s_f1, t.g + 1)
                    op = nc.scalar.copy(f1_raw[:], side[:, 0:P].rearrange("p (b e) -> p b e", b=NB)[:, :, H:2 * H])
                elif name == "x1t":
                    op = nc.scalar.copy(x1T[:], side[:])
                elif name == "q":
                    op = nc.scalar.activation(qT[:], side[:], ACT.Relu, bias=bq_col[:, 0:1])
                elif name == "k":
                    op = nc.scalar.activation(kT[:], side[:], ACT.Relu, bias=bk_col[:, 0:1])
                elif name == "v":
                    if due(t.g - 1):
                        act.wait_ge(s_vb, t.g - 1)
                    op = nc.scalar.copy(v_pre[:], side[:].rearrange("p (b n) -> p b n", b=NB))
                else:
                    at = 2 * int(name[2])
                    if t.prev:
                        act.wait_ge(s_pre, t.g)
                    op = nc.scalar.copy(xw[1 - t.p][:, at:at + 2, :], side[:].rearrange("p (b n) -> p b n", b=2))
                op.then_inc(s_side_read, 1)

            def exp_tile(t, s):
                n = t.tile(s)
                act.wait_ge(s_masked, n + 1)
                if due(n - RING + 1):
                    act.wait_ge(s_flip, n - RING + 1)
                if DENSE <= s < DENSE + NB:
                    i = s - DENSE
                    op = nc.scalar.activation(prob[s % RING][:], neg_h[s % RING][:], ACT.Exp,
                                              bias=d_neg_max[:, i:i + 1], accum_out=d_sums[:, i:i + 1])
                else:
                    h, i = UNITS[s - s % NB], s % NB
                    op = nc.scalar.activation(prob[s % RING][:], neg_h[s % RING][:], ACT.Exp, scale=-1.0,
                                              bias=neg_max[t.p][:, i, h:h + 1], accum_out=sums[t.p][:, i, h:h + 1])
                op.then_inc(s_exp, 1)

            def copy_flipped(t, s):
                act.wait_ge(s_flip, t.tile(s) + 1)
                if s % NB == 0:
                    if 0 <= s < NB and due(t.side_base):
                        act.wait_ge(s_side, t.side_base)
                    if due(t.groups_used(s)):
                        act.wait_ge(s_value, t.groups_used(s))
                nc.scalar.copy(probT[t.group(s)][:, s % NB, :], flip[s % 2][:]).then_inc(s_probT, 1)

            def logits(t, graph, p, h, b):
                u = graph * H + h
                if b == 0:
                    if due(u - 1):
                        act.wait_ge(s_lo, HALVES * (u - 1))
                    if h == 0:
                        act.wait_ge(s_f2_all[p], H * loads(graph, p))
                        act.wait_ge(s_f1, graph + 1)
                nc.scalar.activation(w[h % 2][:, b, :], f2_all[p][:, h, :], ACT.Identity,
                                     scale=row_scale[p][:, b:b + 1], bias=f1[p][:, b, h:h + 1]).then_inc(s_logit, 1)

            for t in turns(act):
                g, q = t.g, 1 - t.p
                for s in range(SLOTS):
                    if s in t.job and t.job[s] not in VECTOR_JOBS:
                        side_out(t, t.job[s])
                    if s == 5 and t.prev:
                        act.wait_ge(s_pre, g)
                        if due(g - 1):
                            act.wait_ge(s_y, g - 1)
                        nc.scalar.activation(th[:], pre[:], ACT.Tanh).then_inc(s_tanh, 1)
                    for unit, b in LOGITS.get(s, ()):
                        if unit < H and t.heads:
                            logits(t, g, t.p, unit, b)
                        elif unit >= H and t.next:
                            logits(t, g + 1, q, unit - H, b)
                    if s == 3 and t.prev:
                        act.wait_ge(s_value, g * H)
                        if due(t.side_base):
                            act.wait_ge(s_side, t.side_base)
                        nc.scalar.copy(headsT_sb[:], headsT[:]).then_inc(s_headsT, 1)
                    if t.has_tile(s):
                        exp_tile(t, s)
                    for r in t.due_now(s, LAG_C):
                        copy_flipped(t, r)
                    if s in ROWSUMS and t.next:
                        for b in ROWSUMS[s]:
                            if b == 0:
                                act.wait_ge(s_adj[q], loads(g + 1, q))
                                if due(2 * (g + 1)):
                                    act.wait_ge(s_rows, 2 * (g + 1))
                            if due(NB * (g + 1) + b):
                                act.wait_ge(s_rowsum, NB * (g + 1) + b)
                            nc.scalar.activation(scrap[:], adj_sb[q][:, b, :], ACT.Identity,
                                                 accum_out=rowsum[:, b:b + 1]).then_inc(s_rowsum, 1)

        @block.vector
        def _(dve):
            def find_zeros(t, s):
                n = t.tile(s)
                dve.wait_ge(s_score, n + 1)
                if due(n - 1):
                    dve.wait_ge(s_masked, n - 1)
                nc.vector.tensor_scalar(zero_pen[s % 2][:], score[s % RING][:], 0.0, -BIG, ALU.is_equal,
                                        ALU.mult).then_inc(s_pen, 1)

            def mask_head(t, s):
                n, m, h, i = t.tile(s), t.head_tile(s), UNITS[s - s % NB], s % NB
                if due(n - RING + 1):
                    dve.wait_ge(s_exp, n - RING + 1)
                dve.wait_ge(s_pen, m + 1)
                dve.nop(nofuse=True)
                nc.vector.tensor_tensor_reduce(neg_h[s % RING][:], score[s % RING][:], zero_pen[s % 2][:], -1.0, BIG,
                                               ALU.add, ALU.min, neg_max[t.p][:, i, h:h + 1]).then_inc(s_masked, 1)

            def mask_dense(t, s):
                n, i = t.tile(s), s - DENSE
                step = 2 * (NB * (t.g - 1) + i)
                dve.wait_ge(s_score, n + 1)
                dve.wait_ge(s_exp, n - RING + 1)
                if i == 0:
                    dve.wait_ge(s_cap, t.g)
                nc.vector.scalar_tensor_tensor(out=neg_h[s % RING][:], in0=score[s % RING][:], scalar=CLAMP_HI,
                                               in1=cap[:, i, :], op0=ALU.min, op1=ALU.min).then_inc(s_dmax, 1)
                dve.wait_ge(s_dmax, step + 1)
                nc.vector.tensor_reduce(d_max[:, i:i + 1], neg_h[s % RING][:], AX_X, ALU.max).then_inc(s_dmax, 1)
                dve.wait_ge(s_dmax, step + 2)
                nc.vector.tensor_scalar(d_neg_max[:, i:i + 1], d_max[:, i:i + 1], -1.0, None,
                                        ALU.mult).then_inc(s_masked, 1)

            def leaky_relu(unit, h, b):
                mine = w[h % 2][:, b, :]
                dve.wait_ge(s_logit, NB * unit + b + 1)
                nc.vector.scalar_tensor_tensor(out=mine, in0=mine, scalar=SLOPE, in1=mine, op0=ALU.mult, op1=ALU.max)\
                    .then_inc(s_lrelu, 1)

            def round_half(unit, h, half_no, free):
                lo, hi = half_no * (NB // HALVES), (half_no + 1) * (NB // HALVES)
                if half_no == 0 and due(free):
                    dve.wait_ge(s_score, free)
                dve.wait_ge(s_lrelu, NB * unit + hi)
                nc.vector.tensor_copy(w_hi[h % 2][:, lo:hi, :], w[h % 2][:, lo:hi, :]).then_inc(s_hi, 1)

            def leaky_at(t, s):
                for unit, b in t.leaky.get(s, ()):
                    if t.next if unit >= H else t.heads:
                        leaky_relu(t.unit(unit), unit % H, b)

            def round_at(t, s):
                unit, half_no = t.round[s]
                if t.next if unit >= H else t.heads:
                    before = {1: -1, 2: 3, 3: 7, H: 11}[unit]
                    round_half(t.unit(unit), unit % H, half_no, t.tile(before) + 1 if t.heads else 0)

            def head_scales(t):
                g, o = t.g, 1 - t.p
                dve.wait_ge(s_exp, t.tile(0))
                if due(g - 1):
                    dve.wait_ge(s_side_read, t.side_base)
                nc.vector.reciprocal(recip[:], sums[o][:]).then_inc(s_recip, 1)
                dve.wait_ge(s_recip, 2 * g - 1)
                nc.vector.scalar_tensor_tensor(out=head_scale[:], in0=neg_max[o][:], scalar=0.5 * BIG, in1=recip[:],
                                               op0=ALU.is_lt, op1=ALU.mult).then_inc(s_recip, 1)

            def row_stats(src, into, total, s_steps, g, blocks):
                for b in blocks:
                    op = nc.vector.bn_stats(into[:, b, :], src[:, b, :])
                if b < NB - 1:
                    return
                op.then_inc(s_steps, 1)
                dve.wait_ge(s_steps, 2 * g - 1)
                dve.nop(nofuse=True)
                for b in range(NB):
                    op = nc.vector.bn_aggr(total[:, b, :], into[:, b, :])
                op.then_inc(s_steps, 1)

            def write_out(graph):
                dve.wait_ge(s_rstd2, graph + 1)
                if due(graph):
                    dve.wait_ge(s_stored, 16 * graph)
                for b in range(NB):
                    op = nc.vector.tensor_scalar(out_sb[:, b, :], y2[:, b, :], mean_var2[:, b, 0:1],
                                                 rstd2[:, b:b + 1], ALU.subtract, ALU.mult)
                op.then_inc(s_out, 1)

            def residual_sum(t):
                q = 1 - t.p
                dve.wait_ge(s_tanh, t.g)
                dve.wait_ge(s_x[q], loads(t.g - 1, q))
                if due(t.g - 1):
                    dve.wait_ge(s_x1, t.g - 1)
                nc.vector.tensor_tensor(y[:], x_sb[q][:], th[:], ALU.add).then_inc(s_y, 1)

            def centre_x1():
                for b in range(NB):
                    op = nc.vector.tensor_scalar(x1[:, b, :], y[:, b, :], mean_var[:, b, 0:1], rstd[:, b:b + 1],
                                                 ALU.subtract, ALU.mult)
                op.then_inc(s_x1, 1)

            def side_out(t, name):
                dve.wait_ge(s_side, t.side[name] + 1)
                if name == "heads":
                    dve.wait_ge(s_recip, 2 * t.g)
                    if due(t.g - 1):
                        dve.wait_ge(s_pre, t.g - 1)
                    nc.vector.tensor_tensor(att[:].rearrange("p b (h d) -> p b h d", h=H),
                                            side[:].rearrange("p (h b d) -> p b h d", h=H, b=NB),
                                            head_scale[:].rearrange("p b (h o) -> p b h o", o=1)
                                            .broadcast_to([P, NB, H, D]), ALU.mult).then_inc(s_side_read, 1)
                else:
                    i = int(name[1])
                    if i == 0:
                        if due(t.g - 1):
                            dve.wait_ge(s_out, t.g - 1)
                    nc.vector.reciprocal(d_recip[:, i:i + 1], d_sums[:, i:i + 1]).then_inc(s_dinv, 1)
                    dve.wait_ge(s_dinv, NB * (t.g - 1) + i + 1)
                    nc.vector.scalar_tensor_tensor(out=y2[:, i, :], in0=side[:, 0:P], scalar=d_recip[:, i:i + 1],
                                                   in1=x1[:, i, :], op0=ALU.mult, op1=ALU.add)\
                        .then_inc(s_side_read, 1)

            nc.vector.memset(half[:], -0.5).then_inc(s_fold, 1)
            nc.vector.memset(w_f[:], 0.0).then_inc(s_fold, 1)
            dve.wait_ge(s_uv, 16 * 3)
            for k in (1, 0):
                nc.vector.tensor_tensor(wuv[:, k, :], wp[:, 0:P], uv_row[:, k, :], ALU.mult).then_inc(s_fold, 1)
            dve.wait_ge(s_fold, 4)
            for at, k in ((0, 1), (H, 0)):
                nc.vector.tensor_reduce(w_f[:, at:at + H], wuv[:, k, :].rearrange("p (h d) -> p h d", h=H), AX_X,
                                        ALU.add).then_inc(s_fold, 1)

            for t in turns(dve):
                g, q = t.g, 1 - t.p
                for s in range(SLOTS):
                    if s == ROW_SCALE and t.next:
                        dve.wait_ge(s_rowsum, NB * (g + 2))
                        if due(g + 1):
                            dve.wait_ge(s_adj_r, g + 1)
                        nc.vector.tensor_scalar(row_zero[:], rowsum[:], 0.0, None, ALU.is_equal).then_inc(s_rows, 1)
                        if t.prev:
                            dve.wait_ge(s_logit, g * H * NB)
                        nc.vector.tensor_scalar(row_scale[q][:], rowsum[:], 0.0, ZERO_ROW, ALU.is_gt,
                                                ALU.max).then_inc(s_rows, 1)
                        dve.wait_ge(s_side_read, t.side["f1"] + 1)
                        dve.wait_ge(s_rows, 2 * (g + 2))
                        nc.vector.tensor_tensor(f1[q][:], f1_raw[:], row_scale[q][:].rearrange("p (b o) -> p b o", o=1)
                                                .broadcast_to([P, NB, H]), ALU.mult).then_inc(s_f1, 1)
                    if s == 0:
                        round_at(t, s)
                    if s == 17 and t.fixed and g < 0:
                        dve.wait_ge(s_weights, weights_loaded)
                        nc.vector.tensor_tensor(bias_row[:], bias_rows[:, 0, :], bias_rows[:, 1, :],
                                                ALU.add).then_inc(s_bias, 1)
                    dense = DENSE <= s < DENSE + NB
                    if t.has_tile(s) and not dense:
                        find_zeros(t, s)
                    leaky_at(t, s)
                    if t.has_tile(s):
                        (mask_dense if dense else mask_head)(t, s)
                    if t.job.get(s) in VECTOR_JOBS:
                        side_out(t, t.job[s])
                    if s > 0 and s in t.round:
                        round_at(t, s)
                    if s == 6 and t.prev:
                        residual_sum(t)
                        dve.wait_ge(s_y, g)
                        if due(g - 1):
                            dve.wait_ge(s_x1, g - 1)
                        row_stats(y, stats, mean_var, s_stats, g, range(NB))
                    if s == 7 and t.prev:
                        dve.wait_ge(s_rstd, g)
                        dve.wait_ge(s_side_read, t.side_base)
                        centre_x1()
                    if s == WRITE_OUT and (not t.fixed or g >= 2):
                        write_out(g - 2)
                    if s == 3 and t.prev:
                        head_scales(t)
                    if s in STATS2 and t.prev:
                        job, blocks = STATS2[s]
                        dve.wait_ge(s_side_read, t.side[job] + 1)
                        row_stats(y2, stats2, mean_var2, s_stats2, g, blocks)
            write_out(GRAPHS - 1)

        @block.gpsimd
        def _(pool):
            def split_lo(unit, h, half_no):
                part = slice(half_no * (NB // HALVES), (half_no + 1) * (NB // HALVES))
                pool.wait_ge(s_hi, HALVES * unit + half_no + 1)
                nc.gpsimd.tensor_tensor(w_lo[h % 2][:, part, :], w[h % 2][:, part, :],
                                        w_hi[h % 2][:, part, :].bitcast(F32), ALU.subtract).then_inc(s_lo, 1)

            def add_biases(t):
                proj = skip[1 - t.p]
                pool.wait_ge(s_side_read, t.side["sp1"] + 1)
                pool.wait_ge(s_bias, 1)
                nc.gpsimd.tensor_tensor(proj, proj, bias_row[:].rearrange("p (o n) -> p o n", o=1)
                                        .broadcast_to([P, NB, P]), ALU.add).then_inc(s_skip, 1)

            def inverse_std(total, shifted, scale, s_steps, s_shift, done, g):
                pool.wait_ge(s_steps, 2 * g)
                pool.nop(nofuse=True)
                nc.gpsimd.tensor_scalar(shifted[:], total[:, :, 1], EPS, None, ALU.add).then_inc(s_shift, 1)
                pool.wait_ge(s_shift, g)
                nc.gpsimd.tensor_tensor(scale[:], shifted[:], half[:], ALU.pow).then_inc(done, 1)

            nc.gpsimd.memset(ident[:], 0.0).then_inc(s_ident, 1)
            pool.wait_ge(s_ident, 1)
            nc.gpsimd.affine_select(out=ident[:], in_=ident[:], compare_op=ALU.not_equal, fill=1.0, base=0,
                                    pattern=[[-1, P]], channel_multiplier=1).then_inc(s_ident, 1)
            pool.wait_ge(s_fold, FOLD_STEPS)

            for t in turns(pool):
                g, q = t.g, 1 - t.p
                if t.heads:
                    split_lo(t.unit(1), 1, 0)
                    split_lo(t.unit(1), 1, 1)
                if t.prev:
                    pool.wait_ge(s_skip, g)
                    pool.wait_ge(s_side_read, t.side["heads"] + 1)
                    if due(g - 1):
                        pool.wait_ge(s_tanh, g - 1)
                    nc.gpsimd.tensor_tensor(pre[:], att[:], skip[q], ALU.add).then_inc(s_pre, 1)
                if t.heads:
                    split_lo(t.unit(2), 2, 0)
                    split_lo(t.unit(2), 2, 1)
                if t.prev:
                    inverse_std(mean_var, var_eps, rstd, s_stats, s_eps, s_rstd, g)
                if t.next:
                    pool.wait_ge(s_rows, 2 * (g + 2))
                    if t.prev:
                        pool.wait_ge(s_score, t.tile(0))
                    pool.nop(nofuse=True)
                    for b in range(NB):
                        op = nc.gpsimd.tensor_scalar(adj_r[q][:, b, :], adj_sb[q][:, b, :], 1.0,
                                                     row_zero[:, b:b + 1], ALU.mult, ALU.add)
                    op.then_inc(s_adj_r, 1)
                if t.next and not (t.fixed and g < 0):
                    add_biases(t)
                if t.heads:
                    split_lo(t.unit(3), 3, 0)
                    split_lo(t.unit(3), 3, 1)
                if t.prev:
                    pool.wait_ge(s_side_read, t.side["v"] + 1)
                    nc.gpsimd.tensor_tensor(v_biased[:], v_pre[:],
                                            bv_row[:].rearrange("p (o n) -> p o n", o=1).broadcast_to([P, NB, P]),
                                            ALU.add).then_inc(s_vb, 1)
                    pool.wait_ge(s_vb, g)
                    pool.wait_ge(s_side, t.side_base)
                    pool.nop(nofuse=True)
                    nc.gpsimd.tensor_scalar(v_sb[:], v_biased[:], 0.0, None, ALU.max).then_inc(s_v, 1)
                if t.next:
                    split_lo(t.unit(H), 0, 0)
                if t.heads:
                    pool.wait_ge(s_adj[t.p], loads(g, t.p))
                    if t.prev:
                        pool.wait_ge(s_masked, t.tile(DENSE + NB - 1) + 1)
                    pool.nop(nofuse=True)
                    nc.gpsimd.tensor_scalar(cap[:], adj_sb[t.p][:], 2 * NEG_PENALTY, -NEG_PENALTY, ALU.mult,
                                            ALU.add).then_inc(s_cap, 1)
                if t.next:
                    split_lo(t.unit(H), 0, 1)
                    if t.fixed and g < 0:
                        add_biases(t)
                if t.prev:
                    inverse_std(mean_var2, var_eps2, rstd2, s_stats2, s_eps2, s_rstd2, g)


def kernel(x, adj, L0_gnn_weight, L0_gnn_weight_u, L0_gnn_weight_v, L0_gnn_bias, L0_gnn_proj_w, L0_gnn_proj_b,
           L1_gnn_Wv, L1_gnn_bv, L1_gnn_Wk, L1_gnn_bk, L1_gnn_Wq, L1_gnn_bq):
    import numpy as np
    import concourse.bacc as bacc
    from concourse.bass_utils import run_bass_kernel_spmd

    def as_laid(a):
        return np.ascontiguousarray(np.asarray(a))

    arrays = {
        "x": as_laid(x),
        "xT": as_laid(np.asarray(x).transpose(0, 2, 1)),
        "adj": as_laid(adj),
        "w0": as_laid(L0_gnn_weight),
        "u0": as_laid(np.asarray(L0_gnn_weight_u).reshape(1, P)),
        "v0": as_laid(np.asarray(L0_gnn_weight_v).reshape(1, P)),
        "bias0": as_laid(np.asarray(L0_gnn_bias).reshape(1, P)),
        "projT": as_laid(np.asarray(L0_gnn_proj_w).T),
        "proj_b": as_laid(np.asarray(L0_gnn_proj_b).reshape(1, P)),
        "wvT": as_laid(np.asarray(L1_gnn_Wv).T),
        "bv": as_laid(np.asarray(L1_gnn_bv).reshape(1, P)),
        "wkT": as_laid(np.asarray(L1_gnn_Wk).T),
        "bk": as_laid(np.asarray(L1_gnn_bk).reshape(P, 1)),
        "wqT": as_laid(np.asarray(L1_gnn_Wq).T),
        "bq": as_laid(np.asarray(L1_gnn_bq).reshape(P, 1)),
    }
    nc = bacc.Bacc("TRN2", target_bir_lowering=False, num_devices=1)
    aps = {k: nc.dram_tensor(f"in_{k}", a.shape, mybir.dt.from_np(a.dtype), kind="ExternalInput").ap()
           for k, a in arrays.items()}
    out = nc.dram_tensor("out", (GRAPHS, N, F), F32, kind="ExternalOutput").ap()
    build(nc, **aps, out=out)
    result = run_bass_kernel_spmd(nc, [{f"in_{k}": a for k, a in arrays.items()}], core_ids=[0])
    return result.results[0]["out"]
```
